# Optimizing a Trainium2 kernel written in Bass

```python
import numpy as np
import jax
import jax.numpy as jnp

def _softmax(x, axis=-1):
    return jax.nn.softmax(x, axis=axis)

def _gelu(x):
    return jax.nn.gelu(x, approximate=True)

def _silu(x):
    return jax.nn.silu(x)

def _sigmoid(x):
    return jax.nn.sigmoid(x)

def _layernorm(x, axis=-1, eps=1e-05):
    m = jnp.mean(x, axis=axis, keepdims=True)
    v = jnp.var(x, axis=axis, keepdims=True)
    return (x - m) / jnp.sqrt(v + eps)

def _scatter_add(tgt, idx, src, axis=0):
    return tgt.at[idx].add(src)

def _segment_sum(src, seg, n):
    return jax.ops.segment_sum(src, seg, n)
kernel_name = 'mk_sandwich_d1_jaxref_r8_5ee7e8'

def setup_inputs(seed: int=0):
    np.random.seed(seed)
    _w = jnp.asarray

    def _L0_attn_setup():
        import jax, jax.numpy as jnp
        import numpy as np
        HEADS = 4
        DIM_HEAD = 32
        EPS = 1e-05
        key = jax.random.key(seed)
        ks = jax.random.split(key, 6)
        b, n, dim = (8, 512, 128)
        hidden = HEADS * DIM_HEAD
        x = jax.random.normal(ks[0], (b, n, dim), dtype=jnp.float32)
        gamma = jnp.ones((1, 1, dim), dtype=jnp.float32)
        beta = jnp.zeros((1, 1, dim), dtype=jnp.float32)
        w_qkv = jax.random.normal(ks[1], (dim, hidden * 3), dtype=jnp.float32) / np.sqrt(dim)
        w_out = jax.random.normal(ks[2], (hidden, dim), dtype=jnp.float32) / np.sqrt(hidden)
        b_out = jnp.zeros((dim,), dtype=jnp.float32)
        return {'x': x, 'gamma': gamma, 'beta': beta, 'w_qkv': w_qkv, 'w_out': w_out, 'b_out': b_out}
    _L0_attn_in = _L0_attn_setup()

    def _L0_ffn_setup():
        import jax, jax.numpy as jnp
        import numpy as np
        NUM_EXPERTS = 8
        HIDDEN = 128
        FFN = 512
        BATCH = 2
        SEQ = 256
        key = jax.random.key(seed)
        k_x, k_g, k_u, k_d = jax.random.split(key, 4)
        scale_in = 1.0 / np.sqrt(HIDDEN)
        scale_mid = 1.0 / np.sqrt(FFN)
        return {'hidden_states': jax.random.normal(k_x, (BATCH, SEQ, HIDDEN), dtype=jnp.float32), 'Wg': jax.random.normal(k_g, (NUM_EXPERTS, HIDDEN, FFN), dtype=jnp.float32) * scale_in, 'Wu': jax.random.normal(k_u, (NUM_EXPERTS, HIDDEN, FFN), dtype=jnp.float32) * scale_in, 'Wd': jax.random.normal(k_d, (NUM_EXPERTS, FFN, HIDDEN), dtype=jnp.float32) * scale_mid}
    _L0_ffn_in = _L0_ffn_setup()
    _d = {'L0_attn_x': _L0_attn_in['x'], 'L0_attn_gamma': _L0_attn_in['gamma'], 'L0_attn_beta': _L0_attn_in['beta'], 'L0_attn_w_qkv': _L0_attn_in['w_qkv'], 'L0_attn_w_out': _L0_attn_in['w_out'], 'L0_attn_b_out': _L0_attn_in['b_out'], 'L0_ffn_Wg': _L0_ffn_in['Wg'], 'L0_ffn_Wu': _L0_ffn_in['Wu'], 'L0_ffn_Wd': _L0_ffn_in['Wd']}
    _x0 = _d['L0_attn_x']
    _d['L0_attn_x'] = jax.random.normal(jax.random.fold_in(jax.random.key(seed), 1), (8, 512, 128), dtype=_x0.dtype)
    del _x0
    return _d

def reference(L0_attn_x, L0_attn_gamma, L0_attn_beta, L0_attn_w_qkv, L0_attn_w_out, L0_attn_b_out, L0_ffn_Wg, L0_ffn_Wu, L0_ffn_Wd):

    def _L0_attn_ref(x, gamma, beta, w_qkv, w_out, b_out):
        import jax, jax.numpy as jnp
        import numpy as np
        HEADS = 4
        DIM_HEAD = 32
        EPS = 1e-05
        b, n, dim = x.shape
        mean = jnp.mean(x, axis=2, keepdims=True)
        var = jnp.var(x, axis=2, keepdims=True)
        xn = (x - mean) / jnp.sqrt(var + EPS) * gamma + beta
        qkv = jnp.einsum('bnc,ck->bnk', xn, w_qkv)
        q, k, v = jnp.split(qkv, 3, axis=2)

        def to_heads(t):
            return t.reshape(b, n, HEADS, DIM_HEAD)
        q, k, v = (to_heads(q), to_heads(k), to_heads(v))
        q = q * DIM_HEAD ** (-0.5)
        k = jax.nn.softmax(k, axis=1)
        context = jnp.einsum('bnhd,bnhe->bhde', k, v)
        out = jnp.einsum('bhde,bnhd->bnhe', context, q)
        out = out.reshape(b, n, HEADS * DIM_HEAD)
        out = jnp.einsum('bnk,kc->bnc', out, w_out) + b_out
        return out + x

    def _L0_ffn_ref(hidden_states, Wg, Wu, Wd):
        import jax, jax.numpy as jnp
        import numpy as np
        NUM_EXPERTS = 8
        HIDDEN = 128
        FFN = 512
        BATCH = 2
        SEQ = 256
        B, S, H = hidden_states.shape
        x = hidden_states.reshape(-1, H)

        def expert_step(acc, w):
            wg, wu, wd = w
            h = jax.nn.silu(x @ wg) * (x @ wu)
            return (acc + h @ wd, None)
        acc, _ = jax.lax.scan(expert_step, jnp.zeros_like(x), (Wg, Wu, Wd))
        return acc.reshape(B, S, H)
    x = L0_attn_x
    x = x + _layernorm(_L0_attn_ref(_layernorm(x, axis=-1), L0_attn_gamma, L0_attn_beta, L0_attn_w_qkv, L0_attn_w_out, L0_attn_b_out), axis=-1)
    x = x + _layernorm(_L0_ffn_ref(_layernorm(x, axis=-1), L0_ffn_Wg, L0_ffn_Wu, L0_ffn_Wd), axis=-1)
    return x

_drawn_inputs = setup_inputs


def setup_inputs(seed=0):
    import zlib

    import numpy as np

    out = dict(_drawn_inputs(seed))
    spreads = {'L0_attn_gamma': (1.0, 0.2), 'L0_attn_beta': (0.0, 0.1), 'L0_attn_b_out': (0.0, 0.1)}
    factors = {}
    for name, (base, spread) in spreads.items():
        noise = np.random.default_rng([zlib.crc32(name.encode()), seed]).standard_normal(out[name].shape)
        drawn = base * np.exp(spread * noise) if base else spread * noise
        out[name] = jnp.asarray(drawn.astype(out[name].dtype))
    for name, factor in factors.items():
        out[name] = (out[name] * factor).astype(out[name].dtype)
    return out
```

```python
from contextlib import ExitStack

import concourse.bass as bass
from concourse import mybir

ALU = mybir.AluOpType
ACT = mybir.ActivationFunctionType
F32 = mybir.dt.float32
F32R = mybir.dt.float32r
AX_X = mybir.AxisListType.X

P = 128
EPS = 1e-5
HEADS = 4


LAG = 3
NGU = 3
NH = 4

PE_AT = {"fin_T": 3, "xn_T": 8, "kT": 10, "E_T": 13, "A": 15, "ctx": 17, "M": 18, "G": 19,
         "attn": 21, "x1n_T": 28}
DVE_AT = {"x_stats": 0, "fin_stats": 4, "fin_scale": 6, "kmax": 11,
          "A": 16, "ctx": 17, "M": 18, "z": 22, "z_stats": 22, "x1_stats": 25, "x1n_lo": 30}
ACT_AT = {"acc": 2, "xn_T": 9, "exp": 12, "E": 14, "G": 20, "x1n_hi": 29}
POOL_AT = {"x_rstd": 1, "xn": 1, "fin_rstd": 5, "fin_out": 7, "z_rstd": 22, "x1": 24, "x1_rstd": 26}


def build(nc, x, gamma, beta, w_qkv, w_out, b_out, Wg, Wu, Wd, out):
    B, N, D = x.shape
    E, _, F = Wg.shape
    J = N // P
    FT = F // P
    STEPS = E * FT
    NW = 3 * E
    DH = D // HEADS
    Q_SCALE = float(DH) ** -0.5

    ctx = ExitStack()
    with ctx:
        def sb(name, shape, dt=F32):
            return ctx.enter_context(nc.sbuf_tensor(name, shape, dt))

        def bank(name):
            return ctx.enter_context(nc.psum_tensor(name, [P, 512], F32))

        def sem(name):
            return ctx.enter_context(nc.semaphore(name))

        x_v = x.rearrange("b (p j) d -> b p j d", j=J)
        out_v = out.rearrange("b (p j) d -> b p j d", j=J)

        ident = sb("ident", [P, P])
        head_mask = sb("head_mask", [P, P])
        expo = sb("expo", [P, 2 * J])
        gamma_bc = sb("gamma_bc", [P, D])
        beta_bc = sb("beta_bc", [P, D])
        bout_bc = sb("bout_bc", [P, D])
        wqkv = sb("wqkv", [P, 3 * D])
        wqT = sb("wqT", [P, D])
        wout = sb("wout", [P, D])
        w_raw = sb("w_raw", [P, 6, F])
        w_hi = [sb(f"w{k}_hi", [P, E, F], F32R) for k in "gud"]
        w_lo = [sb(f"w{k}_lo", [P, E, F], F32R) for k in "gud"]
        x_in = [sb(f"x_in{i}", [P, J, D]) for i in range(2)]
        y = sb("y", [P, J, D])
        yb = sb("yb", [P, J, D])
        xc = sb("xc", [P, J, D])
        xg = sb("xg", [P, J, D])
        xn = sb("xn", [P, J, D])
        xnT = sb("xnT", [P, N])
        kmax_neg = sb("kmax_neg", [P, 1])
        ET = sb("ET", [P, N])
        esum = sb("esum", [P, 1])
        erec = sb("erec", [P, 1])
        Ek = sb("Ek", [P, J, D])
        A_sb = sb("A_sb", [P, D])
        ctxT = sb("ctxT", [P, D])
        M_sb = sb("M_sb", [P, D])
        G_sb = sb("G_sb", [P, D])
        z = sb("z", [P, J, D])
        zn = sb("zn", [P, J, D])
        x1 = [sb(f"x1_{i}", [P, J, D]) for i in range(2)]
        x1n = sb("x1n", [P, J, D])
        x1nT_hi = [sb(f"x1nT_hi{i}", [P, N], F32R) for i in range(2)]
        x1nT_lo = [sb(f"x1nT_lo{i}", [P, N], F32R) for i in range(2)]
        gs = [sb(f"gs{i}", [P, N]) for i in range(NGU)]
        h = [sb(f"h{i}", [P, N]) for i in range(NGU)]
        h_hi = [sb(f"h_hi{i}", [P, N], F32R) for i in range(NH)]
        h_lo = [sb(f"h_lo{i}", [P, N], F32R) for i in range(NH)]
        accT = sb("accT", [P, N])
        fn = sb("fn", [P, J, D])
        res = sb("res", [P, J, D])
        norms = ("x", "z", "x1", "fin")
        st = {k: sb(f"st_{k}", [P, J, 6]) for k in norms}
        mv = {k: sb(f"mv_{k}", [P, J, 2]) for k in norms}
        ve = {k: sb(f"ve_{k}", [P, 2, J]) for k in norms}
        rstd = {k: sb(f"rstd_{k}", [P, 2, J]) for k in norms}

        nm = {k: sb(f"nm_{k}", [P, J]) for k in norms if k != "fin"}

        gate_ps = [bank(f"gate_ps{i}") for i in range(NGU)]
        up_ps = [bank(f"up_ps{i}") for i in range(NGU)]
        acc_ps = bank("acc_ps")
        att_ps = bank("att_ps")
        att_v = att_ps[:, :].rearrange("p (j d) -> p j d", j=J)

        s_const = sem("s_const")
        s_x = [sem(f"s_xload{i}") for i in range(2)]
        s_wraw = [sem(f"s_wraw{i}") for i in range(6)]
        s_store = sem("s_store")
        s_zero = sem("s_zero")
        s_made = sem("s_made")
        s_waited = sem("s_waited")
        s_mask = sem("s_mask")
        s_whi = sem("s_whi")
        s_wlo = sem("s_wlo")
        s_gate = sem("s_gate")
        s_up = sem("s_up")
        s_silu = sem("s_silu")
        s_h = sem("s_h")
        s_hhi = sem("s_hhi")
        s_hlo = sem("s_hlo")
        s_down = sem("s_down")
        s_st = {k: sem(f"s_st_{k}") for k in norms}
        s_mv = {k: sem(f"s_mv_{k}") for k in norms}
        s_ve = {k: sem(f"s_ve_{k}") for k in norms}
        s_rstd = {k: sem(f"s_rstd_{k}") for k in norms}
        s_wqT_ps = sem("s_wqT_ps")
        s_wqT = sem("s_wqT")
        s_y = sem("s_y")
        s_xc = sem("s_xc")
        s_xg = sem("s_xg")
        s_xn = sem("s_xn")
        s_yb = sem("s_yb")
        s_xnT_ps = sem("s_xnT_ps")
        s_xnT = sem("s_xnT")
        s_kT_ps = sem("s_kT_ps")
        s_kmax = sem("s_kmax")
        s_ET = sem("s_ET")
        s_erec = sem("s_erec")
        s_E_ps = sem("s_E_ps")
        s_E = sem("s_E")
        s_A_ps = sem("s_A_ps")
        s_A = sem("s_A")
        s_ctx_ps = sem("s_ctx_ps")
        s_ctx = sem("s_ctx")
        s_M_ps = sem("s_M_ps")
        s_M = sem("s_M")
        s_G_ps = sem("s_G_ps")
        s_G = sem("s_G")
        s_attn_ps = sem("s_attn_ps")
        s_z = sem("s_z")
        s_zn = sem("s_zn")
        s_x1 = sem("s_x1_sum")
        s_x1n = sem("s_x1n")
        s_x1nT_ps = sem("s_x1nT_ps")
        s_x1nT_hi = sem("s_x1nT_hi")
        s_x1nT_lo = sem("s_x1nT_lo")
        s_acc = sem("s_acc")
        s_finT_ps = sem("s_finT_ps")
        s_fn = sem("s_fn")
        s_res = sem("s_res")

        block = ctx.enter_context(nc.Block())

        SPLIT_AT = {(m - 6) * 13 // 10: m for m in range(6, NW)}

        def since(s, n):
            return n if s >= n else s + STEPS - max(r for r in range(STEPS) if r % n == s)

        def wait_alone(eng, semaphore, value):
            eng.wait_ge(semaphore, value)
            eng.sem_inc(s_waited, 1)

        def bodies(eng, body):
            body(0, 0, first=True, last=False)
            with eng.Fori(0, (B - 2) // 2) as i:
                body(i * 2 + 1, 1, first=False, last=False)
                body(i * 2 + 2, 0, first=False, last=False)
            body(B - 1, (B - 1) % 2, first=False, last=True)

        @block.sync
        def _(sp):
            def load_x(c, par):
                sp.dma_start(x_in[par][:, :, :], x_v[c]).then_inc(s_x[par], 16)

            def load_w(m):
                e, k = m // 3, m % 3
                if m >= 6:
                    sp.wait_ge(s_wlo, m - 5)
                src = (Wg, Wu, Wd)[k][e]
                dst = w_raw[:, m % 6, :]
                if k == 2:
                    src = src.rearrange("(t p) d -> p t d", p=P)
                    dst = dst.rearrange("p (t d) -> p t d", d=D)
                sp.dma_start(dst, src).then_inc(s_wraw[m % 6], 16)

            sp.sem_inc(s_store, 16)
            load_x(0, 0)
            sp.dma_start(wqkv[:, :], w_qkv).then_inc(s_const, 16)
            sp.dma_start(gamma_bc[:, :], gamma[0].to_broadcast([P, D])).then_inc(s_const, 16)
            sp.dma_start(beta_bc[:, :], beta[0].to_broadcast([P, D])).then_inc(s_const, 16)
            sp.dma_start(bout_bc[:, :], b_out.rearrange("(a d) -> a d", a=1).to_broadcast([P, D])).then_inc(s_const, 16)
            sp.dma_start(wout[:, :], w_out).then_inc(s_const, 16)
            for m in range(6):
                load_w(m)
            load_x(1, 1)
            for m in range(6, NW):
                load_w(m)

            def store(c):
                sp.wait_ge(s_res, c + 1)
                sp.dma_start(out_v[c], res[:, :, :]).then_inc(s_store, 16)

            def body(b, par, first, last):
                if not first:
                    store(b - 1)
                if not last:
                    sp.wait_ge(s_x1, b + 1)
                    load_x(b + 2, par)

            body(0, 0, True, False)
            with sp.Fori(0, (B - 4) // 2) as i:
                body(i * 2 + 1, 1, False, False)
                body(i * 2 + 2, 0, False, False)
            body(B - 3, 1, False, False)
            store(B - 3)
            store(B - 2)
            store(B - 1)
            sp.wait_ge(s_store, 16 * (B + 1))

        @block.gpsimd
        def _(pool):
            pool.memset(ident[:, :], 0.0).then_inc(s_zero, 1)
            pool.memset(expo[:, :], -0.5).then_inc(s_made, 1)
            pool.wait_ge(s_zero, 1)
            pool.affine_select(out=ident[:, :], in_=ident[:, :], compare_op=ALU.not_equal, fill=1.0,
                               base=0, pattern=[[-1, P]], channel_multiplier=1).then_inc(s_made, 1)
            pool.wait_ge(s_made, 2)

            def rstd_of(k, c):
                wait_alone(pool, s_mv[k], c + 1)
                pool.tensor_scalar(ve[k][:, 0, :], mv[k][:, :, 1], 1.0, EPS, ALU.mult, ALU.add).then_inc(s_ve[k], 1)
                if k != "fin":
                    pool.tensor_scalar(nm[k][:, :], mv[k][:, :, 0], -1.0, 0.0, ALU.mult, ALU.add)
                n = 1
                if k == "x":
                    pool.tensor_scalar(ve[k][:, 1, :], mv[k][:, :, 1], 1.0 + EPS, EPS * EPS,
                                       ALU.mult, ALU.add).then_inc(s_ve[k], 1)
                    n = 2
                pool.wait_ge(s_ve[k], c * n + n)
                pool.tensor_tensor(rstd[k][:, 0:n, :], ve[k][:, 0:n, :],
                                   expo[:, 0:n * J].rearrange("p (a j) -> p a j", j=J),
                                   ALU.pow).then_inc(s_rstd[k], 1)

            def scale_of(k, c, dst, src, done, which=0):
                wait_alone(pool, s_rstd[k], c + 1)
                for j in range(J):
                    last = pool.tensor_scalar(dst[:, j, :], src[:, j, :], nm[k][:, j:j + 1],
                                              rstd[k][:, which, j:j + 1], ALU.add, ALU.mult)
                last.then_inc(done, 1)

            def wide(v):
                return v[:, :].rearrange("p (a d) -> p a d", a=1).to_broadcast([P, J, D])

            def make_xn(c, par):
                if isinstance(c, int) and c == 0:
                    pool.wait_ge(s_const, 16 * 5)
                scale_of("x", c, xc, x_in[par], s_xc, which=1)
                pool.wait_ge(s_xc, c + 1)
                pool.tensor_tensor(xg[:, :, :], xc[:, :, :], wide(gamma_bc), ALU.mult).then_inc(s_xg, 1)
                pool.wait_ge(s_xg, c + 1)
                pool.tensor_tensor(xn[:, :, :], xg[:, :, :], wide(beta_bc), ALU.add).then_inc(s_xn, 1)
                scale_of("x", c, y, x_in[par], s_y)
                pool.wait_ge(s_y, c + 1)
                pool.tensor_tensor(yb[:, :, :], y[:, :, :], wide(bout_bc), ALU.add).then_inc(s_yb, 1)

            def make_x1(c, par):
                scale_of("z", c, zn, z, s_zn)
                pool.wait_ge(s_zn, c + 1)
                pool.tensor_tensor(x1[par][:, :, :], zn[:, :, :], x_in[par][:, :, :], ALU.add).then_inc(s_x1, 1)

            def finish(c, par):
                pool.wait_ge(s_fn, c + 1)
                pool.wait_ge(s_store, (c + 1) * 16)
                pool.tensor_tensor(res[:, :, :], fn[:, :, :], x1[par][:, :, :], ALU.add).then_inc(s_res, 1)

            def attention(at, c, par):
                if at == "x_rstd":
                    rstd_of("x", c)
                if at == "xn":
                    make_xn(c, par)
                if at == "z_rstd":
                    rstd_of("z", c)
                if at == "x1":
                    make_x1(c, par)
                if at == "x1_rstd":
                    rstd_of("x1", c)
                    scale_of("x1", c, x1n, x1[par], s_x1n)

            def body(b, par, first, last):
                for s in range(STEPS):
                    for at, when in POOL_AT.items():
                        if when != s:
                            continue
                        if at == "fin_rstd":
                            if not first:
                                rstd_of("fin", b - 1)
                        elif at == "fin_out":
                            if not first:
                                finish(b - 1, 1 - par)
                        elif not last:
                            attention(at, b + 1, 1 - par)

            for at in ("x_rstd", "xn", "z_rstd", "x1", "x1_rstd"):
                attention(at, 0, 0)
            bodies(pool, body)
            rstd_of("fin", B - 1)
            finish(B - 1, (B - 1) % 2)

        @block.scalar
        def _(act):
            def split_hi(m):
                e, k = m // 3, m % 3
                act.wait_ge(s_wraw[m % 6], 16 * (m // 6 + 1))
                act.activation(w_hi[k][:, e, :], w_raw[:, m % 6, :], ACT.Copy).then_inc(s_whi, 1)

            def attention(at, c, par):
                if at == "xn_T":
                    act.wait_ge(s_xnT_ps, c + 1)
                    act.activation(xnT[:, :], att_ps[:, :], ACT.Copy).then_inc(s_xnT, 1)
                if at == "exp":
                    act.wait_ge(s_kmax, c + 1)
                    act.activation(ET[:, :], att_ps[:, :], ACT.Exp, bias=kmax_neg[:, 0:1], scale=1.0,
                                   accum_out=esum[:, 0:1]).then_inc(s_ET, 1)
                if at == "E":
                    act.wait_ge(s_E_ps, c + 1)
                    act.activation(Ek[:, :, :], att_v, ACT.Copy).then_inc(s_E, 1)
                if at == "G":
                    act.wait_ge(s_G_ps, c + 1)
                    act.activation(G_sb[:, :], att_ps[:, 0:D], ACT.Copy).then_inc(s_G, 1)
                if at == "x1n_hi":
                    act.wait_ge(s_x1nT_ps, c + 1)
                    act.activation(x1nT_hi[par][:, :], att_ps[:, :], ACT.Copy).then_inc(s_x1nT_hi, 1)

            def leave_acc(c):
                act.wait_ge(s_down, c * STEPS + STEPS)
                act.activation(accT[:, :], acc_ps[:, :], ACT.Copy).then_inc(s_acc, 1)

            def h_hi_of(t, s, first):
                act.wait_ge(s_h, t + 1)
                if not (first and s < NH):
                    act.wait_ge(s_down, t - since(s, NH) + 1)
                act.activation(h_hi[s % NH][:, :], h[s % NGU][:, :], ACT.Copy).then_inc(s_hhi, 1)

            def body(b, par, first, last):
                for s in range(STEPS):
                    t = b * STEPS + s
                    act.wait_ge(s_gate, t + 1)
                    if not (first and s < NGU):
                        act.wait_ge(s_h, t - since(s, NGU) + 1)
                    q = s % NGU
                    act.activation(gs[q][:, :], gate_ps[q][:, :], ACT.Silu).then_inc(s_silu, 1)
                    if s or not first:
                        h_hi_of(t - 1, (s - 1) % STEPS, first)
                    if first and s in SPLIT_AT:
                        split_hi(SPLIT_AT[s])
                    for at, when in ACT_AT.items():
                        if when != s:
                            continue
                        if at == "acc":
                            if not first:
                                leave_acc(b - 1)
                        elif not last:
                            attention(at, b + 1, 1 - par)

            act.wait_ge(s_wqT_ps, 1)
            act.activation(wqT[:, :], att_ps[:, 0:D], ACT.Copy).then_inc(s_wqT, 1)
            attention("xn_T", 0, 0)
            attention("exp", 0, 0)
            attention("E", 0, 0)
            for m in range(3):
                split_hi(m)
            attention("G", 0, 0)
            for m in range(3, 6):
                split_hi(m)
            attention("x1n_hi", 0, 0)
            bodies(act, body)
            h_hi_of(B * STEPS - 1, STEPS - 1, False)
            leave_acc(B - 1)

        @block.vector
        def _(dve):
            def split_lo(m):
                e, k = m // 3, m % 3
                dve.wait_ge(s_whi, m + 1)
                dve.tensor_tensor(w_lo[k][:, e, :], w_raw[:, m % 6, :], w_hi[k][:, e, :].bitcast(F32),
                                  ALU.subtract).then_inc(s_wlo, 1)

            def stats_of(k, c, src):
                for j in range(J):
                    last = dve.bn_stats(st[k][:, j, :], src[:, j, :])
                last.then_inc(s_st[k], 1)
                wait_alone(dve, s_st[k], c + 1)
                for j in range(J):
                    last = dve.bn_aggr(mv[k][:, j, :], st[k][:, j, :])
                last.then_inc(s_mv[k], 1)

            def scale_of(k, c, dst, src, done, which=0):
                dve.wait_ge(s_rstd[k], c + 1)
                for j in range(J):
                    last = dve.tensor_scalar(dst[:, j, :], src[:, j, :], mv[k][:, j, 0:1],
                                             rstd[k][:, which, j:j + 1], ALU.subtract, ALU.mult)
                last.then_inc(done, 1)

            def attention(at, c, par):
                if at == "x_stats":
                    dve.wait_ge(s_x[par], (c + 2 - par) * 8)
                    stats_of("x", c, x_in[par])
                if at == "kmax":
                    dve.wait_ge(s_kT_ps, c + 1)
                    dve.tensor_reduce(kmax_neg[:, 0:1], att_ps[:, :], AX_X, ALU.max, negate=True).then_inc(s_kmax, 1)
                if at == "A":
                    dve.wait_ge(s_ET, c + 1)
                    dve.reciprocal(erec[:, :], esum[:, :]).then_inc(s_erec, 1)
                    dve.wait_ge(s_A_ps, c + 1)
                    dve.tensor_copy(A_sb[:, :], att_ps[:, 0:D]).then_inc(s_A, 1)
                if at == "ctx":
                    if isinstance(c, int) and c == 0:
                        dve.wait_ge(s_mask, 2)
                    dve.wait_ge(s_ctx_ps, c + 1)
                    dve.tensor_tensor(ctxT[:, :], att_ps[:, 0:D], head_mask[:, :], ALU.mult).then_inc(s_ctx, 1)
                if at == "M":
                    dve.wait_ge(s_erec, c + 1)
                    dve.wait_ge(s_M_ps, c + 1)
                    dve.tensor_scalar(M_sb[:, :], att_ps[:, 0:D], erec[:, 0:1], Q_SCALE, ALU.mult,
                                      ALU.mult).then_inc(s_M, 1)
                if at == "z":
                    dve.wait_ge(s_yb, c + 1)
                    dve.wait_ge(s_attn_ps, c + 1)
                    dve.tensor_tensor(z[:, :, :], att_v, yb[:, :, :], ALU.add).then_inc(s_z, 1)
                if at == "z_stats":
                    dve.wait_ge(s_z, c + 1)
                    stats_of("z", c, z)
                if at == "x1_stats":
                    dve.wait_ge(s_x1, c + 1)
                    stats_of("x1", c, x1[par])
                if at == "x1n_lo":
                    dve.wait_ge(s_x1nT_hi, c + 1)
                    dve.tensor_tensor(x1nT_lo[par][:, :], att_ps[:, :], x1nT_hi[par][:, :].bitcast(F32),
                                      ALU.subtract).then_inc(s_x1nT_lo, 1)

            def finish(at, c):
                if at == "fin_stats":
                    dve.wait_ge(s_finT_ps, c + 1)
                    stats_of("fin", c, att_v)
                if at == "fin_scale":
                    scale_of("fin", c, fn, att_v, s_fn)

            def h_lo_of(t, s, first):
                dve.wait_ge(s_hhi, t + 1)
                if not (first and s < NH):
                    dve.wait_ge(s_down, t - since(s, NH) + 1)
                dve.tensor_tensor(h_lo[s % NH][:, :], h[s % NGU][:, :], h_hi[s % NH][:, :].bitcast(F32),
                                  ALU.subtract).then_inc(s_hlo, 1)

            def body(b, par, first, last):
                for s in range(STEPS):
                    t = b * STEPS + s
                    dve.wait_ge(s_up, t + 1)
                    dve.wait_ge(s_silu, t + 1)
                    if not (first and s < NGU):
                        dve.wait_ge(s_hhi, t - since(s, NGU) + 1)
                        dve.wait_ge(s_hlo, t - since(s, NGU) + 1)
                    q = s % NGU
                    dve.tensor_tensor(h[q][:, :], gs[q][:, :], up_ps[q][:, :], ALU.mult).then_inc(s_h, 1)
                    if s or not first:
                        h_lo_of(t - 1, (s - 1) % STEPS, first)
                    if first and s in SPLIT_AT:
                        split_lo(SPLIT_AT[s])
                    for at, when in DVE_AT.items():
                        if when != s:
                            continue
                        if at in ("fin_stats", "fin_scale"):
                            if not first:
                                finish(at, b - 1)
                        elif not last:
                            attention(at, b + 1, 1 - par)

            dve.memset(head_mask[:, :], 0.0).then_inc(s_mask, 1)
            dve.wait_ge(s_mask, 1)
            for hd in range(HEADS):
                a = hd * DH
                last = dve.memset(head_mask[a:a + DH, a:a + DH], 1.0)
            last.then_inc(s_mask, 1)
            for at in ("x_stats", "kmax", "A", "ctx", "M"):
                attention(at, 0, 0)
            for m in range(3):
                split_lo(m)
            attention("z", 0, 0)
            attention("z_stats", 0, 0)
            for m in range(3, 6):
                split_lo(m)
            for at in ("x1_stats", "x1n_lo"):
                attention(at, 0, 0)
            bodies(dve, body)
            h_lo_of(B * STEPS - 1, STEPS - 1, False)
            for at in ("fin_stats", "fin_scale"):
                finish(at, B - 1)

        @block.tensor
        def _(pe):
            def products(ps, w_h, w_l, x_h, x_l, start, stop):
                pe.matmul(ps, w_h, x_h, start=start, stop=False)
                pe.matmul(ps, w_h, x_l, start=False, stop=False)
                return pe.matmul(ps, w_l, x_h, start=False, stop=stop)

            def gate_up(t, b, s, par, first):
                e, f = s // FT, s % FT
                q = s % NGU
                cols = slice(f * P, f * P + P)
                if s == 0:
                    pe.wait_ge(s_x1nT_hi, b + 1)
                    pe.wait_ge(s_x1nT_lo, b + 1)
                if first and f == 0:
                    pe.wait_ge(s_whi, 3 * e + 3)
                    pe.wait_ge(s_wlo, 3 * e + 3)
                for k, ps, s_done, s_free in ((0, gate_ps[q], s_gate, s_silu), (1, up_ps[q], s_up, s_h)):
                    if not (first and s < NGU):
                        pe.wait_ge(s_free, t - since(s, NGU) + 1)
                    products(ps[:, :], w_hi[k][:, e, cols], w_lo[k][:, e, cols], x1nT_hi[par][:, :],
                             x1nT_lo[par][:, :], True, True).then_inc(s_done, 1)

            def down(t, s):
                e, f, q = s // FT, s % FT, s % NH
                cols = slice(f * D, f * D + D)
                pe.wait_ge(s_hhi, t + 1)
                pe.wait_ge(s_hlo, t + 1)
                products(acc_ps[:, :], w_hi[2][:, e, cols], w_lo[2][:, e, cols], h_hi[q][:, :], h_lo[q][:, :],
                         s == 0, s == STEPS - 1).then_inc(s_down, 1)

            def transposes(src, s_done):
                for j in range(J):
                    last = pe.transpose(att_ps[:, j * P:j * P + P], src(j), ident[:, :])
                last.then_inc(s_done, 1)

            def attention(at, c, fin_before):
                if at == "xn_T":
                    pe.wait_ge(s_xn, c + 1)
                    if fin_before:
                        pe.wait_ge(s_fn, c - 1)
                    transposes(lambda j: xn[:, j, :], s_xnT_ps)
                if at == "kT":
                    pe.wait_ge(s_xnT, c + 1)
                    pe.matmul(att_ps[:, :], wqkv[:, D:2 * D], xnT[:, :], start=True, stop=True).then_inc(s_kT_ps, 1)
                if at == "E_T":
                    pe.wait_ge(s_ET, c + 1)
                    transposes(lambda j: ET[:, j * P:j * P + P], s_E_ps)
                if at == "A":
                    pe.wait_ge(s_E, c + 1)
                    for j in range(J):
                        last = pe.matmul(att_ps[:, 0:D], xn[:, j, :], Ek[:, j, :], start=(j == 0), stop=(j == J - 1))
                    last.then_inc(s_A_ps, 1)
                if at == "ctx":
                    pe.wait_ge(s_A, c + 1)
                    pe.matmul(att_ps[:, 0:D], wqkv[:, 2 * D:3 * D], A_sb[:, :], start=True, stop=True).then_inc(s_ctx_ps, 1)
                if at == "M":
                    pe.wait_ge(s_ctx, c + 1)
                    pe.matmul(att_ps[:, 0:D], ctxT[:, :], wout[:, :], start=True, stop=True).then_inc(s_M_ps, 1)
                if at == "G":
                    pe.wait_ge(s_M, c + 1)
                    pe.matmul(att_ps[:, 0:D], wqT[:, :], M_sb[:, :], start=True, stop=True).then_inc(s_G_ps, 1)
                if at == "attn":
                    pe.wait_ge(s_G, c + 1)
                    for j in range(J):
                        last = pe.matmul(att_ps[:, j * D:j * D + D], xnT[:, j * P:j * P + P], G_sb[:, :],
                                         start=True, stop=True)
                    last.then_inc(s_attn_ps, 1)
                if at == "x1n_T":
                    pe.wait_ge(s_x1n, c + 1)
                    transposes(lambda j: x1n[:, j, :], s_x1nT_ps)

            def finish(c):
                pe.wait_ge(s_acc, c + 1)
                transposes(lambda j: accT[:, j * P:j * P + P], s_finT_ps)

            def body(b, par, first, last):
                for s in range(STEPS):
                    t = b * STEPS + s
                    gate_up(t, b, s, par, first)
                    if s >= LAG:
                        if s == LAG and not first:
                            pe.wait_ge(s_acc, b)
                        down(t - LAG, s - LAG)
                    elif not first:
                        down(t - LAG, STEPS + s - LAG)
                    for at, when in PE_AT.items():
                        if when != s:
                            continue
                        if at == "fin_T":
                            if not first:
                                finish(b - 1)
                        elif not last:
                            attention(at, b + 1, not first)

            pe.wait_ge(s_made, 2)
            pe.wait_ge(s_const, 16 * 5)
            pe.transpose(att_ps[:, 0:D], wqkv[:, 0:D], ident[:, :]).then_inc(s_wqT_ps, 1)
            pe.wait_ge(s_wqT, 1)
            for at in PE_AT:
                if at != "fin_T":
                    attention(at, 0, False)
            bodies(pe, body)
            for s in range(STEPS - LAG, STEPS):
                down((B - 1) * STEPS + s, s)
            finish(B - 1)


_INS = ['L0_attn_x', 'L0_attn_gamma', 'L0_attn_beta', 'L0_attn_w_qkv', 'L0_attn_w_out', 'L0_attn_b_out',
        'L0_ffn_Wg', 'L0_ffn_Wu', 'L0_ffn_Wd']
_OUTS = [((8, 512, 128), 'float32')]


def kernel(**inputs):
    import numpy as _np
    import concourse.bacc as _bacc
    from concourse import mybir as _mybir
    from concourse.bass_utils import run_bass_kernel_spmd as _run

    nc = _bacc.Bacc("TRN2", target_bir_lowering=False, num_devices=1)
    arrays, args = {}, []
    for name in _INS:
        a = _np.ascontiguousarray(inputs[name])
        arrays[f"in_{name}_dram"] = a
        args.append(nc.dram_tensor(f"in_{name}_dram", a.shape, _mybir.dt.from_np(a.dtype), kind="ExternalInput").ap())
    for i, (shape, dtype) in enumerate(_OUTS):
        dt = _mybir.dt.from_np(_np.dtype(dtype))
        args.append(nc.dram_tensor(f"out_{i}_dram", shape, dt, kind="ExternalOutput").ap())
    build(nc, *args)
    r = _run(nc, [arrays], core_ids=[0])
    got = tuple(r.results[0][f"out_{i}_dram"] for i in range(len(_OUTS)))
    return got[0]
```

```python
from contextlib import ExitStack

import concourse.bass as bass
from concourse import mybir

ALU = mybir.AluOpType
ACT = mybir.ActivationFunctionType
F32 = mybir.dt.float32
F32R = mybir.dt.float32r
AX_X = mybir.AxisListType.X

P = 128
EPS = 1e-5
HEADS = 4


LAG = 3
NGU = 3
NH = 4

FRONT = ("acc", "xn_hi", "xn_lo", "kmax", "E", "A", "ctx", "M", "G_hi", "G_lo", "z", "x1n_hi", "x1n_lo")
PE_AT = {"fin_T": 3, "xn_T": 7, "kT": 8, "E_T": 11, "A": 12, "ctx": 13, "M": 14, "G": 15,
         "attn": 16, "x1n_T": 26}
DVE_AT = {"x_stats": 0, "fin_stats": 4, "fin_scale": 6, "xn_lo": 8, "kmax": 9, "A": 13, "ctx": 14,
          "M": 15, "G_lo": 16, "z": 17, "z_stats": 18, "x1_stats": 22, "x1n_lo": 27}
ACT_AT = {"acc": 3, "xn_hi": 8, "exp": 9, "E": 12, "G_hi": 16, "x1n_hi": 27}
POOL_AT = {"x_rstd": 1, "xn": 1, "fin_rstd": 5, "fin_out": 7, "yb": 9, "z_rstd": 18, "x1": 18, "x1_rstd": 22}

BUSY = {"start": 8, "wqT": 4, "xn_T": 6, "kT": 6, "E_T": 3, "A": 2, "ctx": 2, "M": 2, "G": 2, "attn": 26, "x1n_T": 3}


def build(nc, x, gamma, beta, w_qkv, w_out, b_out, Wg, Wu, Wd, out):
    B, N, D = x.shape
    E, _, F = Wg.shape
    J = N // P
    FT = F // P
    STEPS = E * FT
    NW = 3 * E
    DH = D // HEADS
    Q_SCALE = float(DH) ** -0.5

    ctx = ExitStack()
    with ctx:
        def sb(name, shape, dt=F32):
            return ctx.enter_context(nc.sbuf_tensor(name, shape, dt))

        def bank(name):
            return ctx.enter_context(nc.psum_tensor(name, [P, 512], F32))

        def sem(name):
            return ctx.enter_context(nc.semaphore(name))

        x_v = x.rearrange("b (p j) d -> b p j d", j=J)
        out_v = out.rearrange("b (p j) d -> b p j d", j=J)

        ident = sb("ident", [P, P])
        head_mask = sb("head_mask", [P, P])
        expo = sb("expo", [P, 2 * J])
        gamma_bc = sb("gamma_bc", [P, D])
        beta_bc = sb("beta_bc", [P, D])
        bout_bc = sb("bout_bc", [P, D])
        wqkv = sb("wqkv", [P, 3 * D])
        wqT = sb("wqT", [P, D])
        wk_hi = sb("wk_hi", [P, D], F32R)
        wk_lo = sb("wk_lo", [P, D], F32R)
        wout = sb("wout", [P, D])
        w_raw = sb("w_raw", [P, 6, F])
        w_hi = [sb(f"w{k}_hi", [P, E, F], F32R) for k in "gud"]
        w_lo = [sb(f"w{k}_lo", [P, E, F], F32R) for k in "gud"]
        x_in = [sb(f"x_in{i}", [P, J, D]) for i in range(2)]
        y = sb("y", [P, J, D])
        yb = sb("yb", [P, J, D])
        xc = sb("xc", [P, J, D])
        xg = sb("xg", [P, J, D])
        xn = sb("xn", [P, J, D])
        xnT_hi = sb("xnT_hi", [P, N], F32R)
        xnT_lo = sb("xnT_lo", [P, N], F32R)
        kmax_neg = sb("kmax_neg", [P, 1])
        ET = sb("ET", [P, N])
        esum = sb("esum", [P, 1])
        erec = sb("erec", [P, 1])
        Ek = sb("Ek", [P, J, D])
        A_sb = sb("A_sb", [P, D])
        ctxT = sb("ctxT", [P, D])
        M_sb = sb("M_sb", [P, D])
        G_hi = sb("G_hi", [P, D], F32R)
        G_lo = sb("G_lo", [P, D], F32R)
        z = sb("z", [P, J, D])
        zn = sb("zn", [P, J, D])
        x1 = [sb(f"x1_{i}", [P, J, D]) for i in range(2)]
        x1n = sb("x1n", [P, J, D])
        x1nT_hi = [sb(f"x1nT_hi{i}", [P, N], F32R) for i in range(2)]
        x1nT_lo = [sb(f"x1nT_lo{i}", [P, N], F32R) for i in range(2)]
        gs = [sb(f"gs{i}", [P, N]) for i in range(NGU)]
        h = [sb(f"h{i}", [P, N]) for i in range(NGU)]
        h_hi = [sb(f"h_hi{i}", [P, N], F32R) for i in range(NH)]
        h_lo = [sb(f"h_lo{i}", [P, N], F32R) for i in range(NH)]
        accT = sb("accT", [P, N])
        fn = sb("fn", [P, J, D])
        res = sb("res", [P, J, D])
        norms = ("x", "z", "x1", "fin")
        st = {k: sb(f"st_{k}", [P, J, 6]) for k in norms}
        mv = {k: sb(f"mv_{k}", [P, J, 2]) for k in norms}
        ve = {k: sb(f"ve_{k}", [P, 2, J]) for k in norms}
        rstd = {k: sb(f"rstd_{k}", [P, 2, J]) for k in norms}

        nm = {k: sb(f"nm_{k}", [P, J]) for k in norms if k != "fin"}

        gate_ps = [bank(f"gate_ps{i}") for i in range(NGU)]
        up_ps = [bank(f"up_ps{i}") for i in range(NGU)]
        acc_ps = bank("acc_ps")
        att_ps = bank("att_ps")
        att_v = att_ps[:, :].rearrange("p (j d) -> p j d", j=J)

        first_banks = gate_ps + up_ps[:1]

        s_const = sem("s_const")
        s_x = [sem(f"s_xload{i}") for i in range(2)]
        s_wraw = [sem(f"s_wraw{i}") for i in range(6)]
        s_store = sem("s_store")
        s_zero = sem("s_zero")
        s_made = sem("s_made")
        s_waited = sem("s_waited")
        s_mask = sem("s_mask")
        s_whi = sem("s_whi")
        s_wlo = sem("s_wlo")
        s_gate = sem("s_gate")
        s_up = sem("s_up")
        s_silu = sem("s_silu")
        s_h = sem("s_h")
        s_hhi = sem("s_hhi")
        s_hlo = sem("s_hlo")
        s_down = sem("s_down")
        s_st = {k: sem(f"s_st_{k}") for k in norms}
        s_mv = {k: sem(f"s_mv_{k}") for k in norms}
        s_ve = {k: sem(f"s_ve_{k}") for k in norms}
        s_rstd = {k: sem(f"s_rstd_{k}") for k in norms}
        s_wqT_ps = sem("s_wqT_ps")
        s_wqT = sem("s_wqT")
        s_y = sem("s_y")
        s_xc = sem("s_xc")
        s_xg = sem("s_xg")
        s_xn = sem("s_xn")
        s_yb = sem("s_yb")
        s_xnT_ps = sem("s_xnT_ps")
        s_wk_hi = sem("s_wk_hi")
        s_wk_lo = sem("s_wk_lo")
        s_xnT_hi = sem("s_xnT_hi")
        s_xnT_lo = sem("s_xnT_lo")
        s_kT_ps = sem("s_kT_ps")
        s_kmax = sem("s_kmax")
        s_ET = sem("s_ET")
        s_erec = sem("s_erec")
        s_E_ps = sem("s_E_ps")
        s_E = sem("s_E")
        s_A_ps = sem("s_A_ps")
        s_A = sem("s_A")
        s_ctx_ps = sem("s_ctx_ps")
        s_ctx = sem("s_ctx")
        s_M_ps = sem("s_M_ps")
        s_M = sem("s_M")
        s_G_ps = sem("s_G_ps")
        s_G_hi = sem("s_G_hi")
        s_G_lo = sem("s_G_lo")
        s_attn_ps = sem("s_attn_ps")
        s_z = sem("s_z")
        s_zn = sem("s_zn")
        s_x1 = sem("s_x1_sum")
        s_x1n = sem("s_x1n")
        s_x1nT_ps = sem("s_x1nT_ps")
        s_x1nT_hi = sem("s_x1nT_hi")
        s_x1nT_lo = sem("s_x1nT_lo")
        s_first_xg = sem("s_first_xg")
        s_first_xn = sem("s_first_xn")
        s_first_rstd = sem("s_first_rstd")
        s_first_attn = sem("s_first_attn")
        s_first_z = sem("s_first_z")
        s_first_zc = sem("s_first_zc")
        s_first_x1 = sem("s_first_x1")
        s_first_x1c = sem("s_first_x1c")
        s_first_x1n = sem("s_first_x1n")
        s_last_T = sem("s_last_T")
        s_last_fc = sem("s_last_fc")
        s_last_res = sem("s_last_res")
        s_acc = sem("s_acc")
        s_finT_ps = sem("s_finT_ps")
        s_fn = sem("s_fn")
        s_res = sem("s_res")

        block = ctx.enter_context(nc.Block())

        SPLIT_AT = {(m - 6) * 13 // 10: m for m in range(6, NW)}

        def since(s, n):
            return n if s >= n else s + STEPS - max(r for r in range(STEPS) if r % n == s)

        def wait_alone(eng, semaphore, value):
            eng.wait_ge(semaphore, value)
            eng.sem_inc(s_waited, 1)

        def bodies(eng, body):
            body(0, 0, first=True, last=False)
            with eng.Fori(0, (B - 2) // 2) as i:
                body(i * 2 + 1, 1, first=False, last=False)
                body(i * 2 + 2, 0, first=False, last=False)
            body(B - 1, (B - 1) % 2, first=False, last=True)

        @block.sync
        def _(sp):
            def load_x(c, par):
                sp.dma_start(x_in[par][:, :, :], x_v[c]).then_inc(s_x[par], 16)

            def load_w(m):
                e, k = m // 3, m % 3
                if m >= 6:
                    sp.wait_ge(s_wlo, m - 5)
                src = (Wg, Wu, Wd)[k][e]
                dst = w_raw[:, m % 6, :]
                if k == 2:
                    src = src.rearrange("(t p) d -> p t d", p=P)
                    dst = dst.rearrange("p (t d) -> p t d", d=D)
                sp.dma_start(dst, src).then_inc(s_wraw[m % 6], 16)

            sp.sem_inc(s_store, 16)
            load_x(0, 0)
            sp.dma_start(wqkv[:, :], w_qkv).then_inc(s_const, 16)
            sp.dma_start(gamma_bc[:, :], gamma[0].to_broadcast([P, D])).then_inc(s_const, 16)
            sp.dma_start(beta_bc[:, :], beta[0].to_broadcast([P, D])).then_inc(s_const, 16)
            sp.dma_start(bout_bc[:, :], b_out.rearrange("(a d) -> a d", a=1).to_broadcast([P, D])).then_inc(s_const, 16)
            sp.dma_start(wout[:, :], w_out).then_inc(s_const, 16)
            for m in range(6):
                load_w(m)
            load_x(1, 1)
            for m in range(6, NW):
                load_w(m)

            def store(c):
                sp.wait_ge(s_res, c + 1)
                sp.dma_start(out_v[c], res[:, :, :]).then_inc(s_store, 16)

            def body(b, par, first, last):
                if not first:
                    store(b - 1)
                if first:
                    sp.wait_ge(s_first_x1, J)
                elif not last:
                    sp.wait_ge(s_x1, b)
                if not last:
                    load_x(b + 2, par)

            body(0, 0, True, False)
            with sp.Fori(0, (B - 4) // 2) as i:
                body(i * 2 + 1, 1, False, False)
                body(i * 2 + 2, 0, False, False)
            body(B - 3, 1, False, False)
            store(B - 3)
            store(B - 2)
            for j in range(0, J, 2):
                sp.wait_ge(s_last_res, j + 2)
                sp.dma_start(out_v[B - 1, :, j:j + 2, :], res[:, j:j + 2, :]).then_inc(s_store, 16)
            sp.wait_ge(s_store, 16 * (B + 2))

        @block.gpsimd
        def _(pool):
            pool.memset(ident[:, :], 0.0).then_inc(s_zero, 1)
            pool.memset(expo[:, :], -0.5).then_inc(s_made, 1)
            pool.wait_ge(s_zero, 1)
            pool.affine_select(out=ident[:, :], in_=ident[:, :], compare_op=ALU.not_equal, fill=1.0,
                               base=0, pattern=[[-1, P]], channel_multiplier=1).then_inc(s_made, 1)
            pool.wait_ge(s_made, 2)

            def rstd_of(k, c):
                wait_alone(pool, s_mv[k], c + 1)
                pool.tensor_scalar(ve[k][:, 0, :], mv[k][:, :, 1], 1.0, EPS, ALU.mult, ALU.add).then_inc(s_ve[k], 1)
                if k != "fin":
                    pool.tensor_scalar(nm[k][:, :], mv[k][:, :, 0], -1.0, 0.0, ALU.mult, ALU.add)
                n = 1
                if k == "x":
                    pool.tensor_scalar(ve[k][:, 1, :], mv[k][:, :, 1], 1.0 + EPS, EPS * EPS,
                                       ALU.mult, ALU.add).then_inc(s_ve[k], 1)
                    n = 2
                pool.wait_ge(s_ve[k], c * n + n)
                pool.tensor_tensor(rstd[k][:, 0:n, :], ve[k][:, 0:n, :],
                                   expo[:, 0:n * J].rearrange("p (a j) -> p a j", j=J),
                                   ALU.pow).then_inc(s_rstd[k], 1)

            def scale_of(k, c, dst, src, done, which=0):
                wait_alone(pool, s_rstd[k], c + 1)
                for j in range(J):
                    last = pool.tensor_scalar(dst[:, j, :], src[:, j, :], nm[k][:, j:j + 1],
                                              rstd[k][:, which, j:j + 1], ALU.add, ALU.mult)
                last.then_inc(done, 1)

            def wide(v):
                return v[:, :].rearrange("p (a d) -> p a d", a=1).to_broadcast([P, J, D])

            def make_xn(c, par):
                scale_of("x", c, xc, x_in[par], s_xc, which=1)
                pool.wait_ge(s_xc, c)
                pool.tensor_tensor(xg[:, :, :], xc[:, :, :], wide(gamma_bc), ALU.mult).then_inc(s_xg, 1)
                pool.wait_ge(s_xg, c)
                pool.tensor_tensor(xn[:, :, :], xg[:, :, :], wide(beta_bc), ALU.add).then_inc(s_xn, 1)

            def make_yb(c, par):
                scale_of("x", c, y, x_in[par], s_y)
                pool.wait_ge(s_y, c + 1)
                pool.tensor_tensor(yb[:, :, :], y[:, :, :], wide(bout_bc), ALU.add).then_inc(s_yb, 1)

            def make_x1(c, par):
                scale_of("z", c, zn, z, s_zn)
                pool.wait_ge(s_zn, c)
                pool.tensor_tensor(x1[par][:, :, :], zn[:, :, :], x_in[par][:, :, :], ALU.add).then_inc(s_x1, 1)

            def finish(c, par):
                pool.wait_ge(s_fn, c + 1)
                pool.wait_ge(s_store, (c + 1) * 16)
                pool.tensor_tensor(res[:, :, :], fn[:, :, :], x1[par][:, :, :], ALU.add).then_inc(s_res, 1)

            def attention(at, c, par):
                if at == "x_rstd":
                    rstd_of("x", c)
                if at == "xn":
                    make_xn(c, par)
                if at == "yb":
                    make_yb(c, par)
                if at == "z_rstd":
                    rstd_of("z", c)
                if at == "x1":
                    make_x1(c, par)
                if at == "x1_rstd":
                    rstd_of("x1", c)
                    scale_of("x1", c, x1n, x1[par], s_x1n)

            def body(b, par, first, last):
                for s in range(STEPS):
                    for at, when in POOL_AT.items():
                        if when != s:
                            continue
                        if at == "fin_rstd":
                            if not first:
                                rstd_of("fin", b - 1)
                        elif at == "fin_out":
                            if not first:
                                finish(b - 1, 1 - par)
                        elif not last:
                            attention(at, b + 1, 1 - par)

            def power_of(k, which, done):
                a, b = (1.0 + EPS, EPS * EPS) if which else (1.0, EPS)
                pool.tensor_scalar(ve[k][:, which, :], mv[k][:, :, 1], a, b, ALU.mult, ALU.add).then_inc(s_ve[k], 1)
                pool.wait_ge(s_ve[k], 1 + (k == "x" and not which) + (B - 1) * (k == "fin"))
                pool.tensor_tensor(rstd[k][:, which, :], ve[k][:, which, :], expo[:, 0:J], ALU.pow).then_inc(done, 1)

            pool.wait_ge(s_mv["x"], 1)
            power_of("x", 1, s_rstd["x"])
            pool.tensor_scalar(nm["x"][:, :], mv["x"][:, :, 0], -1.0, 0.0, ALU.mult, ALU.add)
            power_of("x", 0, s_first_rstd)
            pool.wait_ge(s_first_rstd, 1)
            scale_of("x", 0, y, x_in[0], s_y)
            pool.wait_ge(s_const, 16 * 5)
            pool.wait_ge(s_y, 1)
            pool.tensor_tensor(yb[:, :, :], y[:, :, :], wide(bout_bc), ALU.add).then_inc(s_yb, 1)
            pool.wait_ge(s_mv["z"], 1)
            power_of("z", 0, s_rstd["z"])
            pool.wait_ge(s_mv["x1"], 1)
            power_of("x1", 0, s_rstd["x1"])
            bodies(pool, body)
            pool.wait_ge(s_mv["fin"], B)
            power_of("fin", 0, s_rstd["fin"])

        @block.scalar
        def _(act):
            def split_hi(m):
                e, k = m // 3, m % 3
                act.wait_ge(s_wraw[m % 6], 16 * (m // 6 + 1))
                act.activation(w_hi[k][:, e, :], w_raw[:, m % 6, :], ACT.Copy).then_inc(s_whi, 1)

            def attention(at, c, par):
                if at == "xn_hi":
                    act.wait_ge(s_xnT_ps, c + 1)
                    act.activation(xnT_hi[:, :], att_ps[:, :], ACT.Copy).then_inc(s_xnT_hi, 1)
                if at == "exp":
                    act.wait_ge(s_kmax, c + 1)
                    act.activation(ET[:, :], att_ps[:, :], ACT.Exp, bias=kmax_neg[:, 0:1], scale=1.0,
                                   accum_out=esum[:, 0:1]).then_inc(s_ET, 1)
                if at == "E":
                    act.wait_ge(s_E_ps, c + 1)
                    act.activation(Ek[:, :, :], att_v, ACT.Copy).then_inc(s_E, 1)
                if at == "G_hi":
                    act.wait_ge(s_G_ps, c + 1)
                    act.activation(G_hi[:, :], att_ps[:, 0:D], ACT.Copy).then_inc(s_G_hi, 1)
                if at == "x1n_hi":
                    act.wait_ge(s_x1nT_ps, c + 1)
                    act.activation(x1nT_hi[par][:, :], att_ps[:, :], ACT.Copy).then_inc(s_x1nT_hi, 1)

            def leave_acc(c):
                act.wait_ge(s_down, c * STEPS + STEPS)
                act.activation(accT[:, :], acc_ps[:, :], ACT.Copy).then_inc(s_acc, 1)

            def stages(s, b, par, first, last, front):
                for at, when in ACT_AT.items():
                    if when != s or (at in FRONT) != front:
                        continue
                    if at == "acc":
                        if not first:
                            leave_acc(b - 1)
                    elif not last:
                        attention(at, b + 1, 1 - par)

            def h_hi_of(t, s, first):
                act.wait_ge(s_h, t + 1)
                if not (first and s < NH):
                    act.wait_ge(s_down, t - since(s, NH) + 1)
                act.activation(h_hi[s % NH][:, :], h[s % NGU][:, :], ACT.Copy).then_inc(s_hhi, 1)

            def body(b, par, first, last):
                for s in range(STEPS):
                    t = b * STEPS + s
                    stages(s, b, par, first, last, front=True)
                    act.wait_ge(s_gate, t + 1)
                    if not (first and s < NGU):
                        act.wait_ge(s_h, t - since(s, NGU) + 1)
                    q = s % NGU
                    act.activation(gs[q][:, :], gate_ps[q][:, :], ACT.Silu).then_inc(s_silu, 1)
                    if s or not first:
                        h_hi_of(t - 1, (s - 1) % STEPS, first)
                    if first and s in SPLIT_AT:
                        split_hi(SPLIT_AT[s])
                    stages(s, b, par, first, last, front=False)

            act.wait_ge(s_wqT_ps, 1)
            act.activation(wqT[:, :], up_ps[2][:, 0:D], ACT.Copy).then_inc(s_wqT, 1)
            act.activation(wk_hi[:, :], wqkv[:, D:2 * D], ACT.Copy).then_inc(s_wk_hi, 1)
            attention("xn_hi", 0, 0)
            for m in range(3):
                split_hi(m)
            attention("exp", 0, 0)
            attention("E", 0, 0)
            for m in range(3, 6):
                split_hi(m)
            attention("G_hi", 0, 0)
            attention("x1n_hi", 0, 0)
            bodies(act, body)
            h_hi_of(B * STEPS - 1, STEPS - 1, False)
            leave_acc(B - 1)

        @block.vector
        def _(dve):
            def split_lo(m):
                e, k = m // 3, m % 3
                dve.wait_ge(s_whi, m + 1)
                dve.tensor_tensor(w_lo[k][:, e, :], w_raw[:, m % 6, :], w_hi[k][:, e, :].bitcast(F32),
                                  ALU.subtract).then_inc(s_wlo, 1)

            def stats_of(k, c, src):
                for j in range(J):
                    last = dve.bn_stats(st[k][:, j, :], src[:, j, :])
                last.then_inc(s_st[k], 1)
                wait_alone(dve, s_st[k], c + 1)
                for j in range(J):
                    last = dve.bn_aggr(mv[k][:, j, :], st[k][:, j, :])
                last.then_inc(s_mv[k], 1)

            def scale_of(k, c, dst, src, done, which=0):
                dve.wait_ge(s_rstd[k], c + 1)
                for j in range(J):
                    last = dve.tensor_scalar(dst[:, j, :], src[:, j, :], mv[k][:, j, 0:1],
                                             rstd[k][:, which, j:j + 1], ALU.subtract, ALU.mult)
                last.then_inc(done, 1)

            def attention(at, c, par):
                if at == "x_stats":
                    dve.wait_ge(s_x[par], (c + 2 - par) * 8)
                    stats_of("x", c, x_in[par])
                if at == "xn_lo":
                    dve.wait_ge(s_xnT_hi, c + 1)
                    dve.tensor_tensor(xnT_lo[:, :], att_ps[:, :], xnT_hi[:, :].bitcast(F32),
                                      ALU.subtract).then_inc(s_xnT_lo, 1)
                if at == "kmax":
                    dve.wait_ge(s_kT_ps, c + 1)
                    dve.tensor_reduce(kmax_neg[:, 0:1], att_ps[:, :], AX_X, ALU.max, negate=True).then_inc(s_kmax, 1)
                if at == "A":
                    dve.wait_ge(s_ET, c + 1)
                    dve.reciprocal(erec[:, :], esum[:, :]).then_inc(s_erec, 1)
                    dve.wait_ge(s_A_ps, c + 1)
                    dve.tensor_copy(A_sb[:, :], att_ps[:, 0:D]).then_inc(s_A, 1)
                if at == "ctx":
                    if isinstance(c, int) and c == 0:
                        dve.wait_ge(s_mask, 2)
                    dve.wait_ge(s_ctx_ps, c + 1)
                    dve.tensor_tensor(ctxT[:, :], att_ps[:, 0:D], head_mask[:, :], ALU.mult).then_inc(s_ctx, 1)
                if at == "M":
                    dve.wait_ge(s_erec, c + 1)
                    dve.wait_ge(s_M_ps, c + 1)
                    dve.tensor_scalar(M_sb[:, :], att_ps[:, 0:D], erec[:, 0:1], Q_SCALE, ALU.mult,
                                      ALU.mult).then_inc(s_M, 1)
                if at == "G_lo":
                    dve.wait_ge(s_G_hi, c + 1)
                    dve.tensor_tensor(G_lo[:, :], att_ps[:, 0:D], G_hi[:, :].bitcast(F32),
                                      ALU.subtract).then_inc(s_G_lo, 1)
                if at == "z":
                    dve.wait_ge(s_yb, c + 1)
                    dve.wait_ge(s_attn_ps, c)
                    dve.tensor_tensor(z[:, :, :], att_v, yb[:, :, :], ALU.add).then_inc(s_z, 1)
                if at == "z_stats":
                    dve.wait_ge(s_z, c)
                    stats_of("z", c, z)
                if at == "x1_stats":
                    dve.wait_ge(s_x1, c)
                    stats_of("x1", c, x1[par])
                if at == "x1n_lo":
                    dve.wait_ge(s_x1nT_hi, c + 1)
                    dve.tensor_tensor(x1nT_lo[par][:, :], att_ps[:, :], x1nT_hi[par][:, :].bitcast(F32),
                                      ALU.subtract).then_inc(s_x1nT_lo, 1)

            def finish(at, c):
                if at == "fin_stats":
                    dve.wait_ge(s_finT_ps, c + 1)
                    stats_of("fin", c, att_v)
                if at == "fin_scale":
                    scale_of("fin", c, fn, att_v, s_fn)

            def stages(s, b, par, first, last, front):
                for at, when in DVE_AT.items():
                    if when != s or (at in FRONT) != front:
                        continue
                    if at in ("fin_stats", "fin_scale"):
                        if not first:
                            finish(at, b - 1)
                    elif not last:
                        attention(at, b + 1, 1 - par)

            def h_lo_of(t, s, first):
                dve.wait_ge(s_hhi, t + 1)
                if not (first and s < NH):
                    dve.wait_ge(s_down, t - since(s, NH) + 1)
                dve.tensor_tensor(h_lo[s % NH][:, :], h[s % NGU][:, :], h_hi[s % NH][:, :].bitcast(F32),
                                  ALU.subtract).then_inc(s_hlo, 1)

            def body(b, par, first, last):
                for s in range(STEPS):
                    t = b * STEPS + s
                    stages(s, b, par, first, last, front=True)
                    dve.wait_ge(s_up, t + 1)
                    dve.wait_ge(s_silu, t + 1)
                    if not (first and s < NGU):
                        dve.wait_ge(s_hhi, t - since(s, NGU) + 1)
                        dve.wait_ge(s_hlo, t - since(s, NGU) + 1)
                    q = s % NGU
                    dve.tensor_tensor(h[q][:, :], gs[q][:, :], up_ps[q][:, :], ALU.mult).then_inc(s_h, 1)
                    if s or not first:
                        h_lo_of(t - 1, (s - 1) % STEPS, first)
                    if first and s in SPLIT_AT:
                        split_lo(SPLIT_AT[s])
                    stages(s, b, par, first, last, front=False)

            dve.memset(head_mask[:, :], 0.0).then_inc(s_mask, 1)
            dve.wait_ge(s_mask, 1)
            for hd in range(HEADS):
                a = hd * DH
                last = dve.memset(head_mask[a:a + DH, a:a + DH], 1.0)
            last.then_inc(s_mask, 1)

            def aggregate(k, c):
                dve.wait_ge(s_st[k], c + 1)
                for j in range(J):
                    last = dve.bn_aggr(mv[k][:, j, :], st[k][:, j, :])
                last.then_inc(s_mv[k], 1)
                dve.wait_ge(s_mv[k], c + 1)

            def stats_behind(k, make, made):
                for j in range(J + 1):
                    if j < J:
                        make(j)
                    if j:
                        dve.wait_ge(made, j)
                        last = dve.bn_stats(st[k][:, j - 1, :], made_of[k](j - 1))
                last.then_inc(s_st[k], 1)
                aggregate(k, 0)

            made_of = {"z": lambda j: z[:, j, :], "x1": lambda j: x1[0][:, j, :]}

            attention("x_stats", 0, 0)
            dve.wait_ge(s_mv["x"], 1)
            dve.wait_ge(s_const, 16 * 5)
            for j in range(J):
                dve.scalar_tensor_tensor(out=xg[:, j, :], in0=x_in[0][:, j, :], scalar=mv["x"][:, j, 0:1],
                                         in1=gamma_bc[:, :], op0=ALU.subtract, op1=ALU.mult).then_inc(s_first_xg, 1)
            dve.wait_ge(s_wk_hi, 1)
            dve.tensor_tensor(wk_lo[:, :], wqkv[:, D:2 * D], wk_hi[:, :].bitcast(F32), ALU.subtract).then_inc(s_wk_lo, 1)
            dve.wait_ge(s_rstd["x"], 1)
            for j in range(J):
                dve.wait_ge(s_first_xg, j + 1)
                dve.scalar_tensor_tensor(out=xn[:, j, :], in0=xg[:, j, :], scalar=rstd["x"][:, 1, j:j + 1],
                                         in1=beta_bc[:, :], op0=ALU.mult, op1=ALU.add).then_inc(s_first_xn, 1)
            for at in ("xn_lo", "kmax", "A", "ctx", "M", "G_lo"):
                attention(at, 0, 0)
                if at == "kmax":
                    for m in range(3):
                        split_lo(m)
            dve.wait_ge(s_yb, 1)

            def make_z(j):
                dve.wait_ge(s_first_attn, j + 1)
                dve.tensor_tensor(z[:, j, :], first_banks[j][:, 0:D], yb[:, j, :], ALU.add).then_inc(s_first_z, 1)

            def make_x1(j):
                dve.wait_ge(s_first_zc, j + 1)
                dve.scalar_tensor_tensor(out=x1[0][:, j, :], in0=zn[:, j, :], scalar=rstd["z"][:, 0, j:j + 1],
                                         in1=x_in[0][:, j, :], op0=ALU.mult, op1=ALU.add).then_inc(s_first_x1, 1)

            stats_behind("z", make_z, s_first_z)
            for j in range(J):
                dve.tensor_scalar(zn[:, j, :], z[:, j, :], mv["z"][:, j, 0:1], None, ALU.subtract).then_inc(s_first_zc, 1)
            dve.wait_ge(s_rstd["z"], 1)
            stats_behind("x1", make_x1, s_first_x1)
            for j in range(J):
                dve.tensor_scalar(xc[:, j, :], x1[0][:, j, :], mv["x1"][:, j, 0:1], None,
                                  ALU.subtract).then_inc(s_first_x1c, 1)
            dve.wait_ge(s_rstd["x1"], 1)
            for j in range(J):
                dve.wait_ge(s_first_x1c, j + 1)
                dve.tensor_scalar(x1n[:, j, :], xc[:, j, :], rstd["x1"][:, 0, j:j + 1], None,
                                  ALU.mult).then_inc(s_first_x1n, 1)
            attention("x1n_lo", 0, 0)
            for m in range(3, 6):
                split_lo(m)
            bodies(dve, body)
            h_lo_of(B * STEPS - 1, STEPS - 1, False)
            dve.wait_ge(s_res, B - 1)
            for j in range(J):
                dve.wait_ge(s_last_T, j + 1)
                last = dve.bn_stats(st["fin"][:, j, :], first_banks[j][:, 0:D])
            last.then_inc(s_st["fin"], 1)
            aggregate("fin", B - 1)
            for j in range(J):
                dve.tensor_scalar(fn[:, j, :], first_banks[j][:, 0:D], mv["fin"][:, j, 0:1], None,
                                  ALU.subtract).then_inc(s_last_fc, 1)
            dve.wait_ge(s_rstd["fin"], B)
            dve.wait_ge(s_store, 16 * B)
            for j in range(J):
                dve.wait_ge(s_last_fc, j + 1)
                dve.scalar_tensor_tensor(out=res[:, j, :], in0=fn[:, j, :], scalar=rstd["fin"][:, 0, j:j + 1],
                                         in1=x1[(B - 1) % 2][:, j, :], op0=ALU.mult,
                                         op1=ALU.add).then_inc(s_last_res, 1)

        @block.tensor
        def _(pe):
            def products(ps, w_h, w_l, x_h, x_l, start, stop, x_l_made, count):
                pe.matmul(ps, w_h, x_h, start=start, stop=False)
                pe.matmul(ps, w_l, x_h, start=False, stop=False)
                pe.wait_ge(x_l_made, count)
                return pe.matmul(ps, w_h, x_l, start=False, stop=stop)

            def gate_up(t, b, s, par, first):
                e, f = s // FT, s % FT
                q = s % NGU
                cols = slice(f * P, f * P + P)
                if s == 0:
                    pe.wait_ge(s_x1nT_hi, b + 1)
                if first and f == 0:
                    pe.wait_ge(s_whi, 3 * e + 3)
                    pe.wait_ge(s_wlo, 3 * e + 3)
                for k, ps, s_done, s_free in ((0, gate_ps[q], s_gate, s_silu), (1, up_ps[q], s_up, s_h)):
                    if not (first and s < NGU):
                        pe.wait_ge(s_free, t - since(s, NGU) + 1)
                    products(ps[:, :], w_hi[k][:, e, cols], w_lo[k][:, e, cols], x1nT_hi[par][:, :],
                             x1nT_lo[par][:, :], True, True, s_x1nT_lo, b + 1).then_inc(s_done, 1)

            def down(t, s):
                e, f, q = s // FT, s % FT, s % NH
                cols = slice(f * D, f * D + D)
                pe.wait_ge(s_hhi, t + 1)
                products(acc_ps[:, :], w_hi[2][:, e, cols], w_lo[2][:, e, cols], h_hi[q][:, :], h_lo[q][:, :],
                         s == 0, s == STEPS - 1, s_hlo, t + 1).then_inc(s_down, 1)

            def transposes(src, s_done):
                for j in range(J):
                    last = pe.transpose(att_ps[:, j * P:j * P + P], src(j), ident[:, :])
                last.then_inc(s_done, 1)

            def attn_tile(ps, j, c):
                toks = slice(j * P, j * P + P)
                return products(ps, xnT_hi[:, toks], xnT_lo[:, toks], G_hi[:, :], G_lo[:, :], True, True,
                                s_G_lo, c + 1)

            def attention(at, c, fin_before):
                if at == "xn_T":
                    pe.wait_ge(s_xn, c)
                    if fin_before:
                        pe.wait_ge(s_fn, c - 1)
                    transposes(lambda j: xn[:, j, :], s_xnT_ps)
                if at == "kT":
                    pe.wait_ge(s_xnT_hi, c + 1)
                    pe.wait_ge(s_xnT_lo, c + 1)
                    products(att_ps[:, :], wk_hi[:, :], wk_lo[:, :], xnT_hi[:, :], xnT_lo[:, :], True,
                             True, s_xnT_lo, c + 1).then_inc(s_kT_ps, 1)
                if at == "E_T":
                    pe.wait_ge(s_ET, c + 1)
                    transposes(lambda j: ET[:, j * P:j * P + P], s_E_ps)
                if at == "A":
                    pe.wait_ge(s_E, c + 1)
                    for j in range(J):
                        last = pe.matmul(att_ps[:, 0:D], xn[:, j, :], Ek[:, j, :], start=(j == 0), stop=(j == J - 1))
                    last.then_inc(s_A_ps, 1)
                if at == "ctx":
                    pe.wait_ge(s_A, c + 1)
                    pe.matmul(att_ps[:, 0:D], wqkv[:, 2 * D:3 * D], A_sb[:, :], start=True, stop=True).then_inc(s_ctx_ps, 1)
                if at == "M":
                    pe.wait_ge(s_ctx, c + 1)
                    pe.matmul(att_ps[:, 0:D], ctxT[:, :], wout[:, :], start=True, stop=True).then_inc(s_M_ps, 1)
                if at == "G":
                    pe.wait_ge(s_M, c + 1)
                    pe.matmul(att_ps[:, 0:D], wqT[:, :], M_sb[:, :], start=True, stop=True).then_inc(s_G_ps, 1)
                if at == "attn":
                    pe.wait_ge(s_G_hi, c + 1)
                    pe.wait_ge(s_G_lo, c + 1)
                    for j in range(J):
                        last = attn_tile(att_ps[:, j * D:j * D + D], j, c)
                    last.then_inc(s_attn_ps, 1)
                if at == "x1n_T":
                    pe.wait_ge(s_x1n, c)
                    transposes(lambda j: x1n[:, j, :], s_x1nT_ps)

            def finish(c):
                pe.wait_ge(s_acc, c + 1)
                transposes(lambda j: accT[:, j * P:j * P + P], s_finT_ps)

            def body(b, par, first, last):
                for s in range(STEPS):
                    t = b * STEPS + s
                    gate_up(t, b, s, par, first)
                    if s >= LAG:
                        if s == LAG and not first:
                            pe.wait_ge(s_acc, b)
                        down(t - LAG, s - LAG)
                    elif not first:
                        down(t - LAG, STEPS + s - LAG)
                    for at, when in PE_AT.items():
                        if when != s:
                            continue
                        if at == "fin_T":
                            if not first:
                                finish(b - 1)
                        elif not last:
                            attention(at, b + 1, not first)

            def keep_busy(n):
                for _ in range(n):
                    pe.matmul(up_ps[1][:, 0:P], ident[:, :], ident[:, :], start=True, stop=True)

            pe.wait_ge(s_made, 2)
            keep_busy(BUSY["start"])
            pe.wait_ge(s_const, 16 * 5)
            pe.transpose(up_ps[2][:, 0:D], wqkv[:, 0:D], ident[:, :]).then_inc(s_wqT_ps, 1)
            keep_busy(BUSY["wqT"])
            for j in range(J):
                pe.wait_ge(s_first_xn, j + 1)
                last = pe.transpose(att_ps[:, j * P:j * P + P], xn[:, j, :], ident[:, :])
            last.then_inc(s_xnT_ps, 1)
            keep_busy(BUSY["xn_T"])
            pe.wait_ge(s_wk_lo, 1)
            for at in ("kT", "E_T", "A", "ctx", "M", "G"):
                if at == "G":
                    pe.wait_ge(s_wqT, 1)
                attention(at, 0, False)
                keep_busy(BUSY[at])
            pe.wait_ge(s_G_hi, 1)
            for j in range(J):
                attn_tile(first_banks[j][:, 0:D], j, 0).then_inc(s_first_attn, 1)
            keep_busy(BUSY["attn"])
            for j in range(J):
                pe.wait_ge(s_first_x1n, j + 1)
                last = pe.transpose(att_ps[:, j * P:j * P + P], x1n[:, j, :], ident[:, :])
            last.then_inc(s_x1nT_ps, 1)
            keep_busy(BUSY["x1n_T"])
            bodies(pe, body)
            for s in range(STEPS - LAG, STEPS):
                down((B - 1) * STEPS + s, s)
            pe.wait_ge(s_acc, B)
            for j in range(J):
                pe.transpose(first_banks[j][:, 0:P], accT[:, j * P:j * P + P], ident[:, :]).then_inc(s_last_T, 1)


_INS = ['L0_attn_x', 'L0_attn_gamma', 'L0_attn_beta', 'L0_attn_w_qkv', 'L0_attn_w_out', 'L0_attn_b_out',
        'L0_ffn_Wg', 'L0_ffn_Wu', 'L0_ffn_Wd']
_OUTS = [((8, 512, 128), 'float32')]


def kernel(**inputs):
    import numpy as _np
    import concourse.bacc as _bacc
    from concourse import mybir as _mybir
    from concourse.bass_utils import run_bass_kernel_spmd as _run

    nc = _bacc.Bacc("TRN2", target_bir_lowering=False, num_devices=1)
    arrays, args = {}, []
    for name in _INS:
        a = _np.ascontiguousarray(inputs[name])
        arrays[f"in_{name}_dram"] = a
        args.append(nc.dram_tensor(f"in_{name}_dram", a.shape, _mybir.dt.from_np(a.dtype), kind="ExternalInput").ap())
    for i, (shape, dtype) in enumerate(_OUTS):
        dt = _mybir.dt.from_np(_np.dtype(dtype))
        args.append(nc.dram_tensor(f"out_{i}_dram", shape, dt, kind="ExternalOutput").ap())
    build(nc, *args)
    r = _run(nc, [arrays], core_ids=[0])
    got = tuple(r.results[0][f"out_{i}_dram"] for i in range(len(_OUTS)))
    return got[0]
```

```python
from contextlib import ExitStack

import concourse.bass as bass
from concourse import mybir

ALU = mybir.AluOpType
ACT = mybir.ActivationFunctionType
F32 = mybir.dt.float32
F32R = mybir.dt.float32r
AX_X = mybir.AxisListType.X

P = 128
EPS = 1e-5
HEADS = 4


LAG = 3
NGU = 3
NH = 4

FRONT = ("acc", "xn_hi", "xn_lo", "kmax", "E", "A", "ctx", "M", "G", "z", "x1n_hi", "x1n_lo")
PE_AT = {"fin_T": 3, "xn_T": 9, "kT": 10, "E_T": 13, "A": 14, "ctx": 15, "M": 16, "G": 17,
         "attn": 18, "x1n_T": 28}
DVE_AT = {"x_stats": 0, "fin_stats": 4, "fin_scale": 7, "xn_lo": 10, "kmax": 11, "A": 15, "ctx": 16,
          "M": 17, "z": 19, "z_stats": 20, "x1_stats": 24, "x1n_lo": 29}
ACT_AT = {"acc": 3, "xn_hi": 10, "exp": 11, "E": 14, "G": 18, "x1n_hi": 29}
POOL_AT = {"x_rstd": 1, "xn": 1, "fin_rstd": 5, "fin_out": 7, "yb": 9, "xnT": 12, "z_rstd": 20, "x1": 20, "x1_rstd": 24}

BUSY = {"start": 8, "wqT": 4, "xn_T": 3, "kT": 6, "E_T": 3, "A": 2, "ctx": 2, "M": 2, "G": 2, "attn": 26, "x1n_T": 3}


def build(nc, x, gamma, beta, w_qkv, w_out, b_out, Wg, Wu, Wd, out):
    B, N, D = x.shape
    E, _, F = Wg.shape
    J = N // P
    FT = F // P
    STEPS = E * FT
    NW = 3 * E
    DH = D // HEADS
    Q_SCALE = float(DH) ** -0.5

    ctx = ExitStack()
    with ctx:
        def sb(name, shape, dt=F32):
            return ctx.enter_context(nc.sbuf_tensor(name, shape, dt))

        def bank(name):
            return ctx.enter_context(nc.psum_tensor(name, [P, 512], F32))

        def sem(name):
            return ctx.enter_context(nc.semaphore(name))

        x_v = x.rearrange("b (p j) d -> b p j d", j=J)
        out_v = out.rearrange("b (p j) d -> b p j d", j=J)

        ident = sb("ident", [P, P])
        head_mask = sb("head_mask", [P, P])
        expo = sb("expo", [P, 2 * J])
        gamma_bc = sb("gamma_bc", [P, D])
        beta_bc = sb("beta_bc", [P, D])
        bout_bc = sb("bout_bc", [P, D])
        wqkv = sb("wqkv", [P, 3 * D])
        wqT = sb("wqT", [P, D])
        wk_hi = sb("wk_hi", [P, D], F32R)
        wk_lo = sb("wk_lo", [P, D], F32R)
        wout = sb("wout", [P, D])
        w_raw = sb("w_raw", [P, 6, F])
        w_hi = [sb(f"w{k}_hi", [P, E, F], F32R) for k in "gud"]
        w_lo = [sb(f"w{k}_lo", [P, E, F], F32R) for k in "gud"]
        x_in = [sb(f"x_in{i}", [P, J, D]) for i in range(2)]
        y = sb("y", [P, J, D])
        yb = sb("yb", [P, J, D])
        xc = sb("xc", [P, J, D])
        xg = sb("xg", [P, J, D])
        xn = sb("xn", [P, J, D])
        xnT_hi = sb("xnT_hi", [P, N], F32R)
        xnT_lo = sb("xnT_lo", [P, N], F32R)
        xnT = sb("xnT", [P, N])
        kmax_neg = sb("kmax_neg", [P, 1])
        ET = sb("ET", [P, N])
        esum = sb("esum", [P, 1])
        erec = sb("erec", [P, 1])
        Ek = sb("Ek", [P, J, D])
        A_sb = sb("A_sb", [P, D])
        ctxT = sb("ctxT", [P, D])
        M_sb = sb("M_sb", [P, D])
        G_sb = sb("G_sb", [P, D])
        z = sb("z", [P, J, D])
        zn = sb("zn", [P, J, D])
        x1 = [sb(f"x1_{i}", [P, J, D]) for i in range(2)]
        x1n = sb("x1n", [P, J, D])
        x1nT_hi = [sb(f"x1nT_hi{i}", [P, N], F32R) for i in range(2)]
        x1nT_lo = [sb(f"x1nT_lo{i}", [P, N], F32R) for i in range(2)]
        gs = [sb(f"gs{i}", [P, N]) for i in range(NGU)]
        h = [sb(f"h{i}", [P, N]) for i in range(NGU)]
        h_hi = [sb(f"h_hi{i}", [P, N], F32R) for i in range(NH)]
        h_lo = [sb(f"h_lo{i}", [P, N], F32R) for i in range(NH)]
        accT = sb("accT", [P, N])
        fn = sb("fn", [P, J, D])
        res = sb("res", [P, J, D])
        norms = ("x", "z", "x1", "fin")
        st = {k: sb(f"st_{k}", [P, J, 6]) for k in norms}
        mv = {k: sb(f"mv_{k}", [P, J, 2]) for k in norms}
        ve = {k: sb(f"ve_{k}", [P, 2, J]) for k in norms}
        rstd = {k: sb(f"rstd_{k}", [P, 2, J]) for k in norms}

        silu_warm = sb("silu_warm", [P, 1])
        nm = {k: sb(f"nm_{k}", [P, J]) for k in norms if k != "fin"}

        gate_ps = [bank(f"gate_ps{i}") for i in range(NGU)]
        up_ps = [bank(f"up_ps{i}") for i in range(NGU)]
        acc_ps = bank("acc_ps")
        att_ps = bank("att_ps")
        att_v = att_ps[:, :].rearrange("p (j d) -> p j d", j=J)

        first_banks = gate_ps + up_ps[:1]

        s_gamma = sem("s_gamma")
        s_wqkv = sem("s_wqkv")
        s_const = sem("s_const")
        s_x = [sem(f"s_xload{i}") for i in range(2)]
        s_wraw = [sem(f"s_wraw{i}") for i in range(6)]
        s_store = sem("s_store")
        s_zero = sem("s_zero")
        s_made = sem("s_made")
        s_waited = sem("s_waited")
        s_mask = sem("s_mask")
        s_whi = sem("s_whi")
        s_wlo = sem("s_wlo")
        s_late_wlo = sem("s_late_wlo")
        s_gate = sem("s_gate")
        s_up = sem("s_up")
        s_silu = sem("s_silu")
        s_h = sem("s_h")
        s_hhi = sem("s_hhi")
        s_hlo = sem("s_hlo")
        s_down = sem("s_down")
        s_st = {k: sem(f"s_st_{k}") for k in norms}
        s_mv = {k: sem(f"s_mv_{k}") for k in norms}
        s_ve = {k: sem(f"s_ve_{k}") for k in norms}
        s_rstd = {k: sem(f"s_rstd_{k}") for k in norms}
        s_wqT_ps = sem("s_wqT_ps")
        s_wqT = sem("s_wqT")
        s_y = sem("s_y")
        s_xc = sem("s_xc")
        s_xg = sem("s_xg")
        s_xn = sem("s_xn")
        s_yb = sem("s_yb")
        s_xnT_ps = sem("s_xnT_ps")
        s_wk_hi = sem("s_wk_hi")
        s_wk_lo = sem("s_wk_lo")
        s_xnT_hi = sem("s_xnT_hi")
        s_xnT_lo = sem("s_xnT_lo")
        s_xnT = sem("s_xnT")
        s_kT_ps = sem("s_kT_ps")
        s_kmax = sem("s_kmax")
        s_ET = sem("s_ET")
        s_erec = sem("s_erec")
        s_E_ps = sem("s_E_ps")
        s_E = sem("s_E")
        s_A_ps = sem("s_A_ps")
        s_A = sem("s_A")
        s_ctx_ps = sem("s_ctx_ps")
        s_ctx = sem("s_ctx")
        s_M_ps = sem("s_M_ps")
        s_M = sem("s_M")
        s_G_ps = sem("s_G_ps")
        s_G = sem("s_G")
        s_attn_ps = sem("s_attn_ps")
        s_z = sem("s_z")
        s_zn = sem("s_zn")
        s_x1 = sem("s_x1_sum")
        s_x1n = sem("s_x1n")
        s_x1nT_ps = sem("s_x1nT_ps")
        s_x1nT_hi = sem("s_x1nT_hi")
        s_x1nT_lo = sem("s_x1nT_lo")
        s_first_T = sem("s_first_T")
        s_first_T_rest = sem("s_first_T_rest")
        s_first_half = sem("s_first_half")
        s_first_xg = sem("s_first_xg")
        s_first_xn = sem("s_first_xn")
        s_first_rstd = sem("s_first_rstd")
        s_first_attn = sem("s_first_attn")
        s_first_z = sem("s_first_z")
        s_first_zc = sem("s_first_zc")
        s_first_x1 = sem("s_first_x1")
        s_first_x1c = sem("s_first_x1c")
        s_first_x1n = sem("s_first_x1n")
        s_last_T = sem("s_last_T")
        s_last_fc = sem("s_last_fc")
        s_last_res = sem("s_last_res")
        s_acc = sem("s_acc")
        s_finT_ps = sem("s_finT_ps")
        s_fn = sem("s_fn")
        s_res = sem("s_res")

        block = ctx.enter_context(nc.Block())

        HI_AT = {12: 0, 13: 2, 14: 3, 15: 4, 16: 5, 17: 6, 18: 7, 19: 14, 20: 15, 21: 16, 22: 19, 23: 20}
        LO_AT = {12: 0, 13: 7, 14: 8, 15: 10, 16: 11, 17: 12, 18: 13, 19: 15, 20: 16, 21: 17, 22: 21, 23: 22}

        HALF = slice(0, N // 2)
        REST = slice(N // 2, N)
        half_banks = {"xn": (gate_ps[0], gate_ps[1]), "E": (att_ps, up_ps[2]), "x1n": (att_ps, up_ps[2])}
        turn = {"xn": 1, "E": 2, "x1n": 3}

        def split_lo(eng, m, made):
            e, k = m // 3, m % 3
            eng.wait_ge(s_whi, m + 1)
            eng.tensor_tensor(w_lo[k][:, e, :], w_raw[:, m % 6, :], w_hi[k][:, e, :].bitcast(F32),
                              ALU.subtract).then_inc(made, 1)

        def since(s, n):
            return n if s >= n else s + STEPS - max(r for r in range(STEPS) if r % n == s)

        def wait_alone(eng, semaphore, value):
            eng.wait_ge(semaphore, value)
            eng.sem_inc(s_waited, 1)

        def bodies(eng, body):
            body(0, 0, first=True, last=False)
            with eng.Fori(0, (B - 2) // 2) as i:
                body(i * 2 + 1, 1, first=False, last=False)
                body(i * 2 + 2, 0, first=False, last=False)
            body(B - 1, (B - 1) % 2, first=False, last=True)

        @block.sync
        def _(sp):
            def load_x(c, par):
                sp.dma_start(x_in[par][:, :, :], x_v[c]).then_inc(s_x[par], 16)

            def load_w(m):
                e, k = m // 3, m % 3
                if m >= 6:
                    former = m - 6
                    if former < 6:
                        sp.wait_ge(s_wlo, former + 1)
                    else:
                        sp.wait_ge(s_late_wlo, former - 5)
                src = (Wg, Wu, Wd)[k][e]
                dst = w_raw[:, m % 6, :]
                if k == 2:
                    src = src.rearrange("(t p) d -> p t d", p=P)
                    dst = dst.rearrange("p (t d) -> p t d", d=D)
                sp.dma_start(dst, src).then_inc(s_wraw[m % 6], 16)

            sp.sem_inc(s_store, 16)
            load_x(0, 0)
            sp.dma_start(gamma_bc[:, :], gamma[0].to_broadcast([P, D])).then_inc(s_gamma, 16)
            sp.dma_start(wqkv[:, :], w_qkv).then_inc(s_wqkv, 16)
            sp.dma_start(beta_bc[:, :], beta[0].to_broadcast([P, D])).then_inc(s_const, 16)
            sp.dma_start(bout_bc[:, :], b_out.rearrange("(a d) -> a d", a=1).to_broadcast([P, D])).then_inc(s_const, 16)
            sp.dma_start(wout[:, :], w_out).then_inc(s_const, 16)
            for m in range(6):
                load_w(m)
            load_x(1, 1)
            for m in range(6, NW):
                load_w(m)

            def store(c):
                sp.wait_ge(s_res, c + 1)
                sp.dma_start(out_v[c], res[:, :, :]).then_inc(s_store, 16)

            def body(b, par, first, last):
                if not first:
                    store(b - 1)
                if first:
                    sp.wait_ge(s_first_x1, J)
                elif not last:
                    sp.wait_ge(s_x1, b)
                if not last:
                    load_x(b + 2, par)

            body(0, 0, True, False)
            with sp.Fori(0, (B - 4) // 2) as i:
                body(i * 2 + 1, 1, False, False)
                body(i * 2 + 2, 0, False, False)
            body(B - 3, 1, False, False)
            store(B - 3)
            store(B - 2)
            for j in range(0, J, 2):
                sp.wait_ge(s_last_res, j + 2)
                sp.dma_start(out_v[B - 1, :, j:j + 2, :], res[:, j:j + 2, :]).then_inc(s_store, 16)
            sp.wait_ge(s_store, 16 * (B + 2))

        @block.gpsimd
        def _(pool):
            pool.memset(ident[:, :], 0.0).then_inc(s_zero, 1)
            pool.memset(expo[:, :], -0.5).then_inc(s_made, 1)
            pool.wait_ge(s_zero, 1)
            pool.affine_select(out=ident[:, :], in_=ident[:, :], compare_op=ALU.not_equal, fill=1.0,
                               base=0, pattern=[[-1, P]], channel_multiplier=1).then_inc(s_made, 1)
            pool.wait_ge(s_made, 2)

            def rstd_of(k, c):
                wait_alone(pool, s_mv[k], c + 1)
                pool.tensor_scalar(ve[k][:, 0, :], mv[k][:, :, 1], 1.0, EPS, ALU.mult, ALU.add).then_inc(s_ve[k], 1)
                if k != "fin":
                    pool.tensor_scalar(nm[k][:, :], mv[k][:, :, 0], -1.0, 0.0, ALU.mult, ALU.add)
                n = 1
                if k == "x":
                    pool.tensor_scalar(ve[k][:, 1, :], mv[k][:, :, 1], 1.0 + EPS, EPS * EPS,
                                       ALU.mult, ALU.add).then_inc(s_ve[k], 1)
                    n = 2
                pool.wait_ge(s_ve[k], c * n + n)
                pool.tensor_tensor(rstd[k][:, 0:n, :], ve[k][:, 0:n, :],
                                   expo[:, 0:n * J].rearrange("p (a j) -> p a j", j=J),
                                   ALU.pow).then_inc(s_rstd[k], 1)

            def scale_of(k, c, dst, src, done, which=0):
                wait_alone(pool, s_rstd[k], c + 1)
                for j in range(J):
                    last = pool.tensor_scalar(dst[:, j, :], src[:, j, :], nm[k][:, j:j + 1],
                                              rstd[k][:, which, j:j + 1], ALU.add, ALU.mult)
                last.then_inc(done, 1)

            def wide(v):
                return v[:, :].rearrange("p (a d) -> p a d", a=1).to_broadcast([P, J, D])

            def make_xn(c, par):
                scale_of("x", c, xc, x_in[par], s_xc, which=1)
                pool.wait_ge(s_xc, c)
                pool.tensor_tensor(xg[:, :, :], xc[:, :, :], wide(gamma_bc), ALU.mult).then_inc(s_xg, 1)
                pool.wait_ge(s_xg, c)
                pool.tensor_tensor(xn[:, :, :], xg[:, :, :], wide(beta_bc), ALU.add).then_inc(s_xn, 1)

            def whole_xnT(c):
                pool.wait_ge(s_xnT_lo, c + 1)
                pool.tensor_tensor(xnT[:, :], xnT_hi[:, :].bitcast(F32), xnT_lo[:, :].bitcast(F32),
                                   ALU.add).then_inc(s_xnT, 1)

            def make_yb(c, par):
                scale_of("x", c, y, x_in[par], s_y)
                pool.wait_ge(s_y, c + 1)
                pool.tensor_tensor(yb[:, :, :], y[:, :, :], wide(bout_bc), ALU.add).then_inc(s_yb, 1)

            def make_x1(c, par):
                scale_of("z", c, zn, z, s_zn)
                pool.wait_ge(s_zn, c)
                pool.tensor_tensor(x1[par][:, :, :], zn[:, :, :], x_in[par][:, :, :], ALU.add).then_inc(s_x1, 1)

            def finish(c, par):
                pool.wait_ge(s_fn, c + 1)
                pool.wait_ge(s_store, (c + 1) * 16)
                pool.tensor_tensor(res[:, :, :], fn[:, :, :], x1[par][:, :, :], ALU.add).then_inc(s_res, 1)

            def attention(at, c, par):
                if at == "x_rstd":
                    rstd_of("x", c)
                if at == "xn":
                    make_xn(c, par)
                if at == "yb":
                    make_yb(c, par)
                if at == "xnT":
                    whole_xnT(c)
                if at == "z_rstd":
                    rstd_of("z", c)
                if at == "x1":
                    make_x1(c, par)
                if at == "x1_rstd":
                    rstd_of("x1", c)
                    scale_of("x1", c, x1n, x1[par], s_x1n)

            def body(b, par, first, last):
                for s in range(STEPS):
                    for at, when in POOL_AT.items():
                        if when != s:
                            continue
                        if at == "fin_rstd":
                            if not first:
                                rstd_of("fin", b - 1)
                        elif at == "fin_out":
                            if not first:
                                finish(b - 1, 1 - par)
                        elif not last:
                            attention(at, b + 1, 1 - par)
                    for m, when in LO_AT.items():
                        if first and when == s:
                            split_lo(pool, m, s_late_wlo)

            def power_of(k, which, done):
                a, b = (1.0 + EPS, EPS * EPS) if which else (1.0, EPS)
                pool.tensor_scalar(ve[k][:, which, :], mv[k][:, :, 1], a, b, ALU.mult, ALU.add).then_inc(s_ve[k], 1)
                pool.wait_ge(s_ve[k], 1 + (k == "x" and not which) + (B - 1) * (k == "fin"))
                pool.tensor_tensor(rstd[k][:, which, :], ve[k][:, which, :], expo[:, 0:J], ALU.pow).then_inc(done, 1)

            pool.wait_ge(s_mv["x"], 1)
            power_of("x", 1, s_rstd["x"])
            pool.tensor_scalar(nm["x"][:, :], mv["x"][:, :, 0], -1.0, 0.0, ALU.mult, ALU.add)
            power_of("x", 0, s_first_rstd)
            pool.wait_ge(s_first_rstd, 1)
            scale_of("x", 0, y, x_in[0], s_y)
            pool.wait_ge(s_gamma, 16)
            pool.wait_ge(s_const, 16 * 3)
            pool.wait_ge(s_y, 1)
            pool.tensor_tensor(yb[:, :, :], y[:, :, :], wide(bout_bc), ALU.add).then_inc(s_yb, 1)
            pool.wait_ge(s_xnT_hi, 1)
            pool.wait_ge(s_first_half, turn["xn"])
            whole_xnT(0)
            for m in range(6, 9):
                split_lo(pool, m, s_late_wlo)
            pool.wait_ge(s_mv["z"], 1)
            power_of("z", 0, s_rstd["z"])
            split_lo(pool, 9, s_late_wlo)
            pool.wait_ge(s_mv["x1"], 1)
            power_of("x1", 0, s_rstd["x1"])
            for m in range(10, 12):
                split_lo(pool, m, s_late_wlo)
            bodies(pool, body)
            pool.wait_ge(s_mv["fin"], B)
            power_of("fin", 0, s_rstd["fin"])

        @block.scalar
        def _(act):
            def split_hi(m):
                e, k = m // 3, m % 3
                act.wait_ge(s_wraw[m % 6], 16 * (m // 6 + 1))
                act.activation(w_hi[k][:, e, :], w_raw[:, m % 6, :], ACT.Copy).then_inc(s_whi, 1)

            def attention(at, c, par):
                if at == "xn_hi":
                    act.wait_ge(s_xnT_ps, c)
                    act.activation(xnT_hi[:, :], att_ps[:, :], ACT.Copy).then_inc(s_xnT_hi, 1)
                if at == "exp":
                    act.wait_ge(s_kmax, c + 1)
                    act.activation(ET[:, :], att_ps[:, :], ACT.Exp, bias=kmax_neg[:, 0:1], scale=1.0,
                                   accum_out=esum[:, 0:1]).then_inc(s_ET, 1)
                if at == "E":
                    act.wait_ge(s_E_ps, c)
                    act.activation(Ek[:, :, :], att_v, ACT.Copy).then_inc(s_E, 1)
                if at == "G":
                    act.wait_ge(s_G_ps, c + 1)
                    act.activation(G_sb[:, :], att_ps[:, 0:D], ACT.Copy).then_inc(s_G, 1)
                if at == "x1n_hi":
                    act.wait_ge(s_x1nT_ps, c)
                    act.activation(x1nT_hi[par][:, :], att_ps[:, :], ACT.Copy).then_inc(s_x1nT_hi, 1)

            def leave_acc(c):
                act.wait_ge(s_down, c * STEPS + STEPS)
                act.activation(accT[:, :], acc_ps[:, :], ACT.Copy).then_inc(s_acc, 1)

            def stages(s, b, par, first, last, front):
                for at, when in ACT_AT.items():
                    if when != s or (at in FRONT) != front:
                        continue
                    if at == "acc":
                        if not first:
                            leave_acc(b - 1)
                    elif not last:
                        attention(at, b + 1, 1 - par)

            def h_hi_of(t, s, first):
                act.wait_ge(s_h, t + 1)
                if not (first and s < NH):
                    act.wait_ge(s_down, t - since(s, NH) + 1)
                act.activation(h_hi[s % NH][:, :], h[s % NGU][:, :], ACT.Copy).then_inc(s_hhi, 1)

            def body(b, par, first, last):
                for s in range(STEPS):
                    t = b * STEPS + s
                    stages(s, b, par, first, last, front=True)
                    act.wait_ge(s_gate, t + 1)
                    if not (first and s < NGU):
                        act.wait_ge(s_h, t - since(s, NGU) + 1)
                    q = s % NGU
                    act.activation(gs[q][:, :], gate_ps[q][:, :], ACT.Silu).then_inc(s_silu, 1)
                    if s or not first:
                        h_hi_of(t - 1, (s - 1) % STEPS, first)
                    for m, when in HI_AT.items():
                        if first and when == s:
                            split_hi(m)
                    stages(s, b, par, first, last, front=False)

            def high_rest(k, dst, done):
                act.wait_ge(s_first_T_rest, turn[k])
                act.activation(dst, half_banks[k][1][:, HALF], ACT.Copy).then_inc(done, 1)

            act.wait_ge(s_wqT_ps, 1)
            act.activation(wqT[:, :], up_ps[2][:, 0:D], ACT.Copy).then_inc(s_wqT, 1)
            act.activation(wk_hi[:, :], wqkv[:, D:2 * D], ACT.Copy).then_inc(s_wk_hi, 1)
            high_rest("xn", xnT_hi[:, REST], s_xnT_hi)
            for m in range(3):
                split_hi(m)
            attention("exp", 0, 0)
            high_rest("E", Ek[:, J // 2:, :], s_E)
            for m in range(3, 9):
                split_hi(m)
            attention("G", 0, 0)
            for m in range(9, 12):
                split_hi(m)
            act.wait_ge(s_made, 2)
            act.activation(silu_warm[:, :], ident[:, 0:1], ACT.Silu)
            high_rest("x1n", x1nT_hi[0][:, REST], s_x1nT_hi)
            bodies(act, body)
            h_hi_of(B * STEPS - 1, STEPS - 1, False)
            act.wait_ge(s_down, B * STEPS)
            for half in (HALF, REST):
                act.activation(accT[:, half], acc_ps[:, half], ACT.Copy).then_inc(s_acc, 1)

        @block.vector
        def _(dve):
            def stats_of(k, c, src):
                for j in range(J):
                    last = dve.bn_stats(st[k][:, j, :], src[:, j, :])
                last.then_inc(s_st[k], 1)
                wait_alone(dve, s_st[k], c + 1)
                for j in range(J):
                    last = dve.bn_aggr(mv[k][:, j, :], st[k][:, j, :])
                last.then_inc(s_mv[k], 1)

            def scale_of(k, c, dst, src, done, which=0):
                dve.wait_ge(s_rstd[k], c + 1)
                for j in range(J):
                    last = dve.tensor_scalar(dst[:, j, :], src[:, j, :], mv[k][:, j, 0:1],
                                             rstd[k][:, which, j:j + 1], ALU.subtract, ALU.mult)
                last.then_inc(done, 1)

            def attention(at, c, par):
                if at == "x_stats":
                    dve.wait_ge(s_x[par], (c + 2 - par) * 8)
                    stats_of("x", c, x_in[par])
                if at == "xn_lo":
                    dve.wait_ge(s_xnT_hi, c + 1)
                    dve.tensor_tensor(xnT_lo[:, :], att_ps[:, :], xnT_hi[:, :].bitcast(F32),
                                      ALU.subtract).then_inc(s_xnT_lo, 1)
                if at == "kmax":
                    dve.wait_ge(s_kT_ps, c + 1)
                    dve.tensor_reduce(kmax_neg[:, 0:1], att_ps[:, :], AX_X, ALU.max, negate=True).then_inc(s_kmax, 1)
                if at == "A":
                    dve.wait_ge(s_ET, c + 1)
                    dve.reciprocal(erec[:, :], esum[:, :]).then_inc(s_erec, 1)
                    dve.wait_ge(s_A_ps, c + 1)
                    dve.tensor_copy(A_sb[:, :], att_ps[:, 0:D]).then_inc(s_A, 1)
                if at == "ctx":
                    if isinstance(c, int) and c == 0:
                        dve.wait_ge(s_mask, 2)
                    dve.wait_ge(s_ctx_ps, c + 1)
                    dve.tensor_tensor(ctxT[:, :], att_ps[:, 0:D], head_mask[:, :], ALU.mult).then_inc(s_ctx, 1)
                if at == "M":
                    dve.wait_ge(s_erec, c + 1)
                    dve.wait_ge(s_M_ps, c + 1)
                    dve.tensor_scalar(M_sb[:, :], att_ps[:, 0:D], erec[:, 0:1], Q_SCALE, ALU.mult,
                                      ALU.mult).then_inc(s_M, 1)
                if at == "z":
                    dve.wait_ge(s_yb, c + 1)
                    dve.wait_ge(s_attn_ps, c)
                    dve.tensor_tensor(z[:, :, :], att_v, yb[:, :, :], ALU.add).then_inc(s_z, 1)
                if at == "z_stats":
                    dve.wait_ge(s_z, c)
                    stats_of("z", c, z)
                if at == "x1_stats":
                    dve.wait_ge(s_x1, c)
                    stats_of("x1", c, x1[par])
                if at == "x1n_lo":
                    dve.wait_ge(s_x1nT_hi, c + 1)
                    dve.tensor_tensor(x1nT_lo[par][:, :], att_ps[:, :], x1nT_hi[par][:, :].bitcast(F32),
                                      ALU.subtract).then_inc(s_x1nT_lo, 1)

            def finish(at, c):
                if at == "fin_stats":
                    dve.wait_ge(s_finT_ps, c + 1)
                    stats_of("fin", c, att_v)
                if at == "fin_scale":
                    scale_of("fin", c, fn, att_v, s_fn)

            def stages(s, b, par, first, last, front):
                for at, when in DVE_AT.items():
                    if when != s or (at in FRONT) != front:
                        continue
                    if at in ("fin_stats", "fin_scale"):
                        if not first:
                            finish(at, b - 1)
                    elif not last:
                        attention(at, b + 1, 1 - par)

            def h_lo_of(t, s, first):
                dve.wait_ge(s_hhi, t + 1)
                if not (first and s < NH):
                    dve.wait_ge(s_down, t - since(s, NH) + 1)
                dve.tensor_tensor(h_lo[s % NH][:, :], h[s % NGU][:, :], h_hi[s % NH][:, :].bitcast(F32),
                                  ALU.subtract).then_inc(s_hlo, 1)

            def body(b, par, first, last):
                for s in range(STEPS):
                    t = b * STEPS + s
                    stages(s, b, par, first, last, front=True)
                    dve.wait_ge(s_up, t + 1)
                    dve.wait_ge(s_silu, t + 1)
                    if not (first and s < NGU):
                        dve.wait_ge(s_hhi, t - since(s, NGU) + 1)
                        dve.wait_ge(s_hlo, t - since(s, NGU) + 1)
                    q = s % NGU
                    dve.tensor_tensor(h[q][:, :], gs[q][:, :], up_ps[q][:, :], ALU.mult).then_inc(s_h, 1)
                    if s or not first:
                        h_lo_of(t - 1, (s - 1) % STEPS, first)
                    stages(s, b, par, first, last, front=False)

            dve.memset(head_mask[:, :], 0.0).then_inc(s_mask, 1)
            dve.wait_ge(s_mask, 1)
            for hd in range(HEADS):
                a = hd * DH
                last = dve.memset(head_mask[a:a + DH, a:a + DH], 1.0)
            last.then_inc(s_mask, 1)

            def aggregate(k, c):
                dve.wait_ge(s_st[k], c + 1)
                for j in range(J):
                    last = dve.bn_aggr(mv[k][:, j, :], st[k][:, j, :])
                last.then_inc(s_mv[k], 1)
                dve.wait_ge(s_mv[k], c + 1)

            def stats_behind(k, make, made):
                for j in range(J + 1):
                    if j < J:
                        make(j)
                    if j:
                        dve.wait_ge(made, j)
                        last = dve.bn_stats(st[k][:, j - 1, :], made_of[k](j - 1))
                last.then_inc(s_st[k], 1)
                aggregate(k, 0)

            def high_half(k, dst):
                dve.wait_ge(s_first_T, turn[k])
                dve.tensor_copy(dst, half_banks[k][0][:, HALF]).then_inc(s_first_half, 1)

            def low(k, hi, lo, rest_made, done):
                for cols, bank_of, made, count in ((HALF, 0, s_first_half, turn[k]), (REST, 1, rest_made, 1)):
                    dve.wait_ge(made, count)
                    last = dve.tensor_tensor(lo[:, cols], half_banks[k][bank_of][:, HALF],
                                             hi[:, cols].bitcast(F32), ALU.subtract)
                last.then_inc(done, 1)

            made_of = {"z": lambda j: z[:, j, :], "x1": lambda j: x1[0][:, j, :]}

            attention("x_stats", 0, 0)
            dve.wait_ge(s_mv["x"], 1)
            dve.wait_ge(s_gamma, 16)
            for j in range(J):
                dve.scalar_tensor_tensor(out=xg[:, j, :], in0=x_in[0][:, j, :], scalar=mv["x"][:, j, 0:1],
                                         in1=gamma_bc[:, :], op0=ALU.subtract, op1=ALU.mult).then_inc(s_first_xg, 1)
            dve.wait_ge(s_const, 16 * 3)
            dve.wait_ge(s_rstd["x"], 1)
            for j in range(J):
                dve.wait_ge(s_first_xg, j + 1)
                dve.scalar_tensor_tensor(out=xn[:, j, :], in0=xg[:, j, :], scalar=rstd["x"][:, 1, j:j + 1],
                                         in1=beta_bc[:, :], op0=ALU.mult, op1=ALU.add).then_inc(s_first_xn, 1)
            dve.wait_ge(s_wk_hi, 1)
            dve.tensor_tensor(wk_lo[:, :], wqkv[:, D:2 * D], wk_hi[:, :].bitcast(F32), ALU.subtract).then_inc(s_wk_lo, 1)
            high_half("xn", xnT_hi[:, HALF])
            low("xn", xnT_hi, xnT_lo, s_xnT_hi, s_xnT_lo)
            for at in ("kmax", "A", "ctx", "M"):
                if at == "A":
                    high_half("E", Ek[:, 0:J // 2, :])
                    split_lo(dve, 2, s_wlo)
                attention(at, 0, 0)
                if at == "kmax":
                    for m in range(2):
                        split_lo(dve, m, s_wlo)
                if at in ("A", "ctx", "M"):
                    split_lo(dve, ("A", "ctx", "M").index(at) + 3, s_wlo)
            dve.wait_ge(s_yb, 1)

            def make_z(j):
                dve.wait_ge(s_first_attn, j + 1)
                dve.tensor_tensor(z[:, j, :], first_banks[j][:, 0:D], yb[:, j, :], ALU.add).then_inc(s_first_z, 1)

            def make_x1(j):
                dve.wait_ge(s_first_zc, j + 1)
                dve.scalar_tensor_tensor(out=x1[0][:, j, :], in0=zn[:, j, :], scalar=rstd["z"][:, 0, j:j + 1],
                                         in1=x_in[0][:, j, :], op0=ALU.mult, op1=ALU.add).then_inc(s_first_x1, 1)

            stats_behind("z", make_z, s_first_z)
            for j in range(J):
                dve.tensor_scalar(zn[:, j, :], z[:, j, :], mv["z"][:, j, 0:1], None, ALU.subtract).then_inc(s_first_zc, 1)
            dve.wait_ge(s_rstd["z"], 1)
            stats_behind("x1", make_x1, s_first_x1)
            for j in range(J):
                dve.tensor_scalar(xc[:, j, :], x1[0][:, j, :], mv["x1"][:, j, 0:1], None,
                                  ALU.subtract).then_inc(s_first_x1c, 1)
            dve.wait_ge(s_rstd["x1"], 1)
            for j in range(J):
                dve.wait_ge(s_first_x1c, j + 1)
                dve.tensor_scalar(x1n[:, j, :], xc[:, j, :], rstd["x1"][:, 0, j:j + 1], None,
                                  ALU.mult).then_inc(s_first_x1n, 1)
            high_half("x1n", x1nT_hi[0][:, HALF])
            low("x1n", x1nT_hi[0], x1nT_lo[0], s_x1nT_hi, s_x1nT_lo)
            bodies(dve, body)
            h_lo_of(B * STEPS - 1, STEPS - 1, False)
            dve.wait_ge(s_res, B - 1)
            for j in range(J):
                dve.wait_ge(s_last_T, j + 1)
                last = dve.bn_stats(st["fin"][:, j, :], first_banks[j][:, 0:D])
            last.then_inc(s_st["fin"], 1)
            aggregate("fin", B - 1)
            for j in range(J):
                dve.tensor_scalar(fn[:, j, :], first_banks[j][:, 0:D], mv["fin"][:, j, 0:1], None,
                                  ALU.subtract).then_inc(s_last_fc, 1)
            dve.wait_ge(s_rstd["fin"], B)
            dve.wait_ge(s_store, 16 * B)
            for j in range(J):
                dve.wait_ge(s_last_fc, j + 1)
                dve.scalar_tensor_tensor(out=res[:, j, :], in0=fn[:, j, :], scalar=rstd["fin"][:, 0, j:j + 1],
                                         in1=x1[(B - 1) % 2][:, j, :], op0=ALU.mult,
                                         op1=ALU.add).then_inc(s_last_res, 1)

        @block.tensor
        def _(pe):
            def products(ps, w_h, w_l, x_h, x_l, start, stop, x_l_made, count):
                pe.matmul(ps, w_h, x_h, start=start, stop=False)
                pe.matmul(ps, w_l, x_h, start=False, stop=False)
                pe.wait_ge(x_l_made, count)
                return pe.matmul(ps, w_h, x_l, start=False, stop=stop)

            def gate_up(t, b, s, par, first):
                e, f = s // FT, s % FT
                q = s % NGU
                cols = slice(f * P, f * P + P)
                if s == 0:
                    pe.wait_ge(s_x1nT_hi, b + 1)
                if first and f == 0:
                    pe.wait_ge(s_whi, 3 * e + 3)
                    if e < 2:
                        pe.wait_ge(s_wlo, 3 * e + 3)
                    else:
                        pe.wait_ge(s_late_wlo, 3 * e + 3 - 6)
                if first and s == 0:
                    halves = [(w_hi[k][:, e, cols], w_lo[k][:, e, cols], ps[q][:, :], done)
                              for k, ps, done in ((0, gate_ps, s_gate), (1, up_ps, s_up))]
                    for hi, lo, ps, _ in halves:
                        pe.matmul(ps, hi, x1nT_hi[par][:, :], start=True, stop=False)
                        pe.matmul(ps, lo, x1nT_hi[par][:, :], start=False, stop=False)
                    pe.wait_ge(s_x1nT_lo, 1)
                    for hi, _, ps, done in halves:
                        pe.matmul(ps, hi, x1nT_lo[par][:, :], start=False, stop=True).then_inc(done, 1)
                    return
                for k, ps, s_done, s_free in ((0, gate_ps[q], s_gate, s_silu), (1, up_ps[q], s_up, s_h)):
                    if not (first and s < NGU):
                        pe.wait_ge(s_free, t - since(s, NGU) + 1)
                    products(ps[:, :], w_hi[k][:, e, cols], w_lo[k][:, e, cols], x1nT_hi[par][:, :],
                             x1nT_lo[par][:, :], True, True, s_x1nT_lo, b + 1).then_inc(s_done, 1)

            def down(t, s):
                e, f, q = s // FT, s % FT, s % NH
                cols = slice(f * D, f * D + D)
                pe.wait_ge(s_hhi, t + 1)
                products(acc_ps[:, :], w_hi[2][:, e, cols], w_lo[2][:, e, cols], h_hi[q][:, :], h_lo[q][:, :],
                         s == 0, s == STEPS - 1, s_hlo, t + 1).then_inc(s_down, 1)

            def transposes(src, s_done):
                for j in range(J):
                    last = pe.transpose(att_ps[:, j * P:j * P + P], src(j), ident[:, :])
                last.then_inc(s_done, 1)

            def attn_tile(ps, j):
                toks = slice(j * P, j * P + P)
                return pe.matmul(ps, xnT[:, toks], G_sb[:, :], start=True, stop=True)

            def attention(at, c, fin_before):
                if at == "xn_T":
                    pe.wait_ge(s_xn, c)
                    if fin_before:
                        pe.wait_ge(s_fn, c - 1)
                    transposes(lambda j: xn[:, j, :], s_xnT_ps)
                if at == "kT":
                    pe.wait_ge(s_xnT_hi, c + 1)
                    if not (isinstance(c, int) and c == 0):
                        pe.wait_ge(s_xnT_lo, c + 1)
                    products(att_ps[:, :], wk_hi[:, :], wk_lo[:, :], xnT_hi[:, :], xnT_lo[:, :], True,
                             True, s_xnT_lo, c + 1).then_inc(s_kT_ps, 1)
                if at == "E_T":
                    pe.wait_ge(s_ET, c + 1)
                    transposes(lambda j: ET[:, j * P:j * P + P], s_E_ps)
                if at == "A":
                    pe.wait_ge(s_E, c + 1)
                    for j in range(J):
                        last = pe.matmul(att_ps[:, 0:D], xn[:, j, :], Ek[:, j, :], start=(j == 0), stop=(j == J - 1))
                    last.then_inc(s_A_ps, 1)
                if at == "ctx":
                    pe.wait_ge(s_A, c + 1)
                    pe.matmul(att_ps[:, 0:D], wqkv[:, 2 * D:3 * D], A_sb[:, :], start=True, stop=True).then_inc(s_ctx_ps, 1)
                if at == "M":
                    pe.wait_ge(s_ctx, c + 1)
                    pe.matmul(att_ps[:, 0:D], ctxT[:, :], wout[:, :], start=True, stop=True).then_inc(s_M_ps, 1)
                if at == "G":
                    pe.wait_ge(s_M, c + 1)
                    pe.matmul(att_ps[:, 0:D], wqT[:, :], M_sb[:, :], start=True, stop=True).then_inc(s_G_ps, 1)
                if at == "attn":
                    pe.wait_ge(s_G, c + 1)
                    pe.wait_ge(s_xnT, c + 1)
                    for j in range(J):
                        last = attn_tile(att_ps[:, j * D:j * D + D], j)
                    last.then_inc(s_attn_ps, 1)
                if at == "x1n_T":
                    pe.wait_ge(s_x1n, c)
                    transposes(lambda j: x1n[:, j, :], s_x1nT_ps)

            def finish(c):
                pe.wait_ge(s_acc, c + 1)
                transposes(lambda j: accT[:, j * P:j * P + P], s_finT_ps)

            def body(b, par, first, last):
                for s in range(STEPS):
                    t = b * STEPS + s
                    gate_up(t, b, s, par, first)
                    if s >= LAG:
                        if s == LAG and not first:
                            pe.wait_ge(s_acc, b)
                        down(t - LAG, s - LAG)
                    elif not first:
                        down(t - LAG, STEPS + s - LAG)
                    for at, when in PE_AT.items():
                        if when != s:
                            continue
                        if at == "fin_T":
                            if not first:
                                finish(b - 1)
                        elif not last:
                            attention(at, b + 1, not first)

            def keep_busy(n):
                for _ in range(n):
                    pe.matmul(up_ps[1][:, 0:P], ident[:, :], ident[:, :], start=True, stop=True)

            def first_transposes(k, src, made=None):
                for j in range(J):
                    if made is not None:
                        pe.wait_ge(made, j + 1)
                    half, col = j * 2 // J, j % (J // 2) * P
                    last = pe.transpose(half_banks[k][half][:, col:col + P], src(j), ident[:, :])
                    if j == J // 2 - 1:
                        last.then_inc(s_first_T, 1)
                last.then_inc(s_first_T_rest, 1)

            pe.wait_ge(s_made, 2)
            keep_busy(BUSY["start"])
            pe.wait_ge(s_wqkv, 16)
            pe.transpose(up_ps[2][:, 0:D], wqkv[:, 0:D], ident[:, :]).then_inc(s_wqT_ps, 1)
            keep_busy(BUSY["wqT"])
            first_transposes("xn", lambda j: xn[:, j, :], s_first_xn)
            keep_busy(BUSY["xn_T"])
            pe.wait_ge(s_wk_lo, 1)
            for at in ("kT", "E_T", "A", "ctx", "M", "G"):
                if at in ("kT", "A"):
                    pe.wait_ge(s_first_half, turn["xn" if at == "kT" else "E"])
                if at == "G":
                    pe.wait_ge(s_wqT, 1)
                if at == "E_T":
                    pe.wait_ge(s_ET, 1)
                    first_transposes("E", lambda j: ET[:, j * P:j * P + P])
                else:
                    attention(at, 0, False)
                keep_busy(BUSY[at])
            pe.wait_ge(s_G, 1)
            pe.wait_ge(s_xnT, 1)
            for j in range(J):
                attn_tile(first_banks[j][:, 0:D], j).then_inc(s_first_attn, 1)
            keep_busy(BUSY["attn"])
            first_transposes("x1n", lambda j: x1n[:, j, :], s_first_x1n)
            keep_busy(BUSY["x1n_T"])
            pe.wait_ge(s_first_half, turn["x1n"])
            bodies(pe, body)
            for s in range(STEPS - LAG, STEPS):
                down((B - 1) * STEPS + s, s)
            for j in range(J):
                pe.wait_ge(s_acc, B + j * 2 // J)
                pe.transpose(first_banks[j][:, 0:P], accT[:, j * P:j * P + P], ident[:, :]).then_inc(s_last_T, 1)


_INS = ['L0_attn_x', 'L0_attn_gamma', 'L0_attn_beta', 'L0_attn_w_qkv', 'L0_attn_w_out', 'L0_attn_b_out',
        'L0_ffn_Wg', 'L0_ffn_Wu', 'L0_ffn_Wd']
_OUTS = [((8, 512, 128), 'float32')]


def kernel(**inputs):
    import numpy as _np
    import concourse.bacc as _bacc
    from concourse import mybir as _mybir
    from concourse.bass_utils import run_bass_kernel_spmd as _run

    nc = _bacc.Bacc("TRN2", target_bir_lowering=False, num_devices=1)
    arrays, args = {}, []
    for name in _INS:
        a = _np.ascontiguousarray(inputs[name])
        arrays[f"in_{name}_dram"] = a
        args.append(nc.dram_tensor(f"in_{name}_dram", a.shape, _mybir.dt.from_np(a.dtype), kind="ExternalInput").ap())
    for i, (shape, dtype) in enumerate(_OUTS):
        dt = _mybir.dt.from_np(_np.dtype(dtype))
        args.append(nc.dram_tensor(f"out_{i}_dram", shape, dt, kind="ExternalOutput").ap())
    build(nc, *args)
    r = _run(nc, [arrays], core_ids=[0])
    got = tuple(r.results[0][f"out_{i}_dram"] for i in range(len(_OUTS)))
    return got[0]
```
